# Optimizing a Trainium2 kernel written in Bass

```python
import numpy as np
import jax
import jax.numpy as jnp

def _softmax(x, axis=-1):
    return jax.nn.softmax(x, axis=axis)

def _gelu(x):
    return jax.nn.gelu(x, approximate=True)

def _silu(x):
    return jax.nn.silu(x)

def _sigmoid(x):
    return jax.nn.sigmoid(x)

def _layernorm(x, axis=-1, eps=1e-05):
    m = jnp.mean(x, axis=axis, keepdims=True)
    v = jnp.var(x, axis=axis, keepdims=True)
    return (x - m) / jnp.sqrt(v + eps)

def _scatter_add(tgt, idx, src, axis=0):
    return tgt.at[idx].add(src)

def _segment_sum(src, seg, n):
    return jax.ops.segment_sum(src, seg, n)
kernel_name = 'mk_adaln_ffn_d1_seqx_r4_a2b83c'

def setup_inputs(seed: int=0):
    np.random.seed(seed)
    _w = jnp.asarray

    def _rec_inputs():
        import jax
        import jax.numpy as jnp
        _rk = jax.random.key(seed)
        x = -7.109e-05 + 0.9999 * jax.random.normal(jax.random.fold_in(_rk, 1), (32, 64, 512), jnp.float32)
        _lenS = 64 - jax.random.randint(jax.random.fold_in(_rk, 7), (32,), 0, max(1, 64 // 4) + 1, jnp.int32)
        _lenS2 = 64 - jax.random.randint(jax.random.fold_in(_rk, 8), (32,), 0, max(1, 64 // 4) + 1, jnp.int32)
        itok_B_1_198 = jax.random.randint(jax.random.fold_in(_rk, 11), (32,), 1, 199, jnp.int32)
        return (x, itok_B_1_198)
    x, itok_B_1_198 = _rec_inputs()

    def _L0_cond_setup():
        import jax, jax.numpy as jnp
        import numpy as np
        B, C, T = (128, 64, 512)
        S, D = (200, 64)
        key = jax.random.key(seed)
        k1, k2, k3 = jax.random.split(key, 3)
        x = jax.random.normal(k1, (B, C, T), dtype=jnp.float32)
        conditions = jax.random.randint(k2, (B,), 0, S, dtype=jnp.int64)
        weights = jax.random.normal(k3, (S, C, D), dtype=jnp.float32) / jnp.sqrt(jnp.float32(C))
        return {'x': x, 'conditions': conditions, 'weights': weights}
    _L0_cond_all = _L0_cond_setup()
    _L0_cond_in = {k: v for k, v in _L0_cond_all.items() if k in ('weights',)}
    del _L0_cond_all

    def _L0_ffn_setup():
        import jax, jax.numpy as jnp
        import numpy as np
        E = 8
        CAPACITY_FACTOR = 1.25
        B, T, H, I = (4, 256, 512, 352)
        key = jax.random.key(seed)
        k0, k1, k2, k3, k4 = jax.random.split(key, 5)
        x = jax.random.normal(k0, (B, T, H), jnp.float32)
        Wr = jax.random.normal(k1, (E, H), jnp.float32) * 0.02
        Wg = jax.random.normal(k2, (E, I, H), jnp.float32) * 0.02
        Wu = jax.random.normal(k3, (E, I, H), jnp.float32) * 0.02
        Wd = jax.random.normal(k4, (E, H, I), jnp.float32) * 0.02
        return {'x': x, 'Wr': Wr, 'Wg': Wg, 'Wu': Wu, 'Wd': Wd}
    _L0_ffn_all = _L0_ffn_setup()
    _L0_ffn_in = {k: v for k, v in _L0_ffn_all.items() if k in ('Wr', 'Wg', 'Wu', 'Wd')}
    del _L0_ffn_all
    return {'x': x, 'itok_B_1_198': itok_B_1_198, 'L0_cond_weights': _L0_cond_in['weights'], 'L0_ffn_Wr': _L0_ffn_in['Wr'], 'L0_ffn_Wg': _L0_ffn_in['Wg'], 'L0_ffn_Wu': _L0_ffn_in['Wu'], 'L0_ffn_Wd': _L0_ffn_in['Wd']}

def reference(x, itok_B_1_198, L0_cond_weights, L0_ffn_Wr, L0_ffn_Wg, L0_ffn_Wu, L0_ffn_Wd):
    import jax
    import jax.numpy as jnp

    def _L0_cond_ref(x, conditions, weights):
        import jax, jax.numpy as jnp
        import numpy as np
        B, C, T = (128, 64, 512)
        S, D = (200, 64)
        w = weights[conditions]
        return jnp.einsum('bct,bcd->bdt', x, w)

    def _L0_ffn_ref(x, Wr, Wg, Wu, Wd):
        import jax, jax.numpy as jnp
        import numpy as np
        E = 8
        CAPACITY_FACTOR = 1.25
        B, T, H, I = (4, 256, 512, 352)
        Bb, Tt, Hh = x.shape
        N = Bb * Tt
        cap = max(1, int(CAPACITY_FACTOR * (N * 2 / E)))
        xf = x.reshape(N, Hh)
        logits = jnp.einsum('nh,eh->ne', xf, Wr)
        gate = jax.nn.softmax(logits, axis=-1)
        top2_val, top2_idx = jax.lax.top_k(gate, 2)
        flat_idx = jnp.concatenate([top2_idx[:, 0], top2_idx[:, 1]])
        flat_val = jnp.concatenate([top2_val[:, 0], top2_val[:, 1]])
        onehot = jax.nn.one_hot(flat_idx, E, dtype=jnp.int32)
        rank = (jnp.cumsum(onehot, axis=0) * onehot).sum(-1)
        keep = rank <= cap
        w_assign = jnp.where(keep, flat_val, 0.0)
        tok = jnp.tile(jnp.arange(N), 2)
        comb = jnp.zeros((N, E), x.dtype).at[tok, flat_idx].add(w_assign)
        g = jax.nn.silu(jnp.einsum('nh,eih->eni', xf, Wg))
        u = jnp.einsum('nh,eih->eni', xf, Wu)
        out_e = jnp.einsum('eni,ehi->enh', g * u, Wd)
        y = jnp.einsum('ne,enh->nh', comb, out_e)
        return y.reshape(Bb, Tt, Hh)
    x = x + _L0_ffn_ref(_L0_cond_ref(x, itok_B_1_198, L0_cond_weights), L0_ffn_Wr, L0_ffn_Wg, L0_ffn_Wu, L0_ffn_Wd)
    return x

_drawn_inputs = setup_inputs


def setup_inputs(seed=0):
    import zlib

    import numpy as np

    out = dict(_drawn_inputs(seed))
    spreads = {}
    factors = {'L0_cond_weights': 4.589,
     'L0_ffn_Wr': 5.386,
     'L0_ffn_Wg': 4.656,
     'L0_ffn_Wu': 4.544,
     'L0_ffn_Wd': 4.542}
    for name, (base, spread) in spreads.items():
        noise = np.random.default_rng([zlib.crc32(name.encode()), seed]).standard_normal(out[name].shape)
        drawn = base * np.exp(spread * noise) if base else spread * noise
        out[name] = jnp.asarray(drawn.astype(out[name].dtype))
    for name, factor in factors.items():
        out[name] = (out[name] * factor).astype(out[name].dtype)
    return out
```

```python
from contextlib import ExitStack

import concourse.bass as bass
from concourse import mybir

B, C, D, H = 32, 64, 64, 512
N = B * D
S = 200
E, I = 8, 352
TOP = 2
CAP = int(1.25 * (N * TOP / E))
P = 128
TT = N // P
KH = H // P
KI = (I + P - 1) // P
IP = KI * P
IR = I - (KI - 1) * P
TPE = CAP // P
NT = E * TPE
A = TOP * TT
FAR = 100000

UNIT = [(k * 2 * I, (k + 1) * 2 * I) for k in range(KH)] + [(KH * 2 * I, KH * 2 * I + KI * H)]
NU = len(UNIT)
DOWN = UNIT[-1][0]
WC = UNIT[-1][1]

XR = 4

PASS = 2 * TPE
FIRST = TPE + 1
PASSES = (NT - FIRST) // PASS

F32 = mybir.dt.float32
F32R = mybir.dt.float32r
BF16 = mybir.dt.bfloat16
I32 = mybir.dt.int32
U32 = mybir.dt.uint32
ALU = mybir.AluOpType
ACT = mybir.ActivationFunctionType
AX = mybir.AxisListType.X


def build(nc, x, cond, wcond, wr, wg, wu, wd, out):
    xf_dram = nc.dram_tensor("xf_dram", (N, H), F32, kind="Internal").ap()
    ctx = ExitStack()
    with ctx:
        def sb(name, shape, dt=F32):
            return ctx.enter_context(nc.sbuf_tensor(name, shape, dt))

        def pb(name):
            return ctx.enter_context(nc.psum_tensor(name, [P, 512], F32))

        def sem(name):
            return ctx.enter_context(nc.semaphore(name))

        ident = sb("ident", [P, P])
        upper = sb("upper", [P, P], BF16)
        ones = sb("ones", [P, P], BF16)
        iota_e = sb("iota_e", [P, E])
        iota_p = sb("iota_p", [P, P])
        iota_t = sb("iota_t", [P, NT])
        row_in_c = sb("row_in_c", [P, 1])
        token1 = sb("token1", [P, TT])
        spare = sb("spare", [P, NT])
        carry = sb("carry", [P, E, A])
        zeros = sb("zeros", [P, H])

        condb = sb("condb", [P, TT], I32)
        cidx = sb("cidx", [P, TT], U32)
        wc_sb = sb("wc_sb", [P, TT, D])
        wbd = sb("wbd", [P, XR, 2 * D])
        wr_sb = sb("wr_sb", [P, KH, E])
        x_sb = sb("x_sb", [P, TT, H])
        xf_sb = sb("xf_sb", [P, XR, H])
        xfT = sb("xfT", [P, 2, H])
        lg = sb("lg", [P, TT, E])
        mx = sb("mx", [P, TT])
        ex = sb("ex", [P, TT, E])
        sm = sb("sm", [P, TT])
        gate = sb("gate", [P, TT, E])
        v8 = sb("v8", [P, TT, 8])
        i8 = sb("i8", [P, TT, 8], U32)
        choice = sb("choice", [P, TOP, TT])
        val = sb("val", [P, TOP, TT])
        tok1 = sb("tok1", [P, TOP, TT])
        oh = sb("oh", [P, E, A], BF16)
        run = sb("run", [P, E, A])
        rk = sb("rk", [P, E, A])
        r1 = sb("r1", [P, A])
        over = sb("over", [P, A])
        slot_f = sb("slot_f", [P, A])
        slot = sb("slot", [P, A], I32)
        slot_i = sb("slot_i", [P, 2, A], I32)
        slot_tp = sb("slot_tp", [P, 2, A])
        pick_t = sb("pick_t", [P, A, NT])
        what = sb("what", [P, A, 2 * NT])
        empty = sb("empty", [P, NT])
        src_row = sb("src_row", [P, NT], U32)
        dst_row = sb("dst_row", [P, NT], U32)
        w_slot = sb("w_slot", [P, NT])

        raw = sb("raw", [P, WC])
        whi = sb("whi", [P, 2, WC], F32R)
        wlo = sb("wlo", [P, 2, WC], F32R)
        tiles = sb("tiles", [P, 2 * TPE * H])
        xg = tiles[:, 0:TPE * H].rearrange("p (t h) -> p t h", h=H)
        y_sb = tiles[:, TPE * H:].rearrange("p (t h) -> p t h", h=H)
        pick_p = tiles[:, 0:A * P].rearrange("p (a q) -> p a q", q=P)
        xhi = sb("xhi", [P, 2, H], F32R)
        xlo = sb("xlo", [P, 2, H], F32R)
        g_sb = sb("g_sb", [P, I])
        h_sb = sb("h_sb", [P, IP])
        hhi = sb("hhi", [P, IP], F32R)
        hlo = sb("hlo", [P, IP], F32R)

        bank = [pb(f"bank{n}") for n in range(8)]
        ps_xf = bank[0:2]
        ps_t = bank[2:4]
        ps_lg = bank[4]
        ps_rank = bank[1]
        ps_slot = bank[3]
        ps_gate, ps_up, ps_hT, ps_xT, ps_y = bank[5], bank[6], bank[7], bank[2], bank[0]

        consts = sem("consts")
        cond_in = sem("cond_in")
        cidx_ok = sem("cidx_ok")
        wr_in = sem("wr_in")
        zeros_ok = sem("zeros_ok")
        wc_in = [sem(f"wc_in{n}") for n in range(XR)]
        x_in = [sem(f"x_in{n}") for n in range(XR)]
        wbd_ok = sem("wbd_ok")
        xf_ps = sem("xf_ps")
        xf_ok = sem("xf_ok")
        xf_out = [sem(f"xf_out{n}") for n in range(XR)]
        t_ps = sem("t_ps")
        xfT_ok = sem("xfT_ok")
        lg_ps = sem("lg_ps")
        sub_ok = sem("sub_ok")
        ex_ok = sem("ex_ok")
        route = sem("route")
        oh_ok = sem("oh_ok")
        rank_ps = sem("rank_ps")
        pick_ok = sem("pick_ok")
        slot_ps = sem("slot_ps")
        lists_ok = sem("lists_ok")
        out_init = sem("out_init")
        raw_in = [sem(f"raw_in{u}") for u in range(NU)]
        pad_ok = sem("pad_ok")
        whi_ok = sem("whi_ok")
        wlo0_ok = sem("wlo0_ok")
        wlo_ok = sem("wlo_ok")
        xg_in = [sem(f"xg_in{n}") for n in range(TPE)]
        xT_ps = sem("xT_ps")
        xhi_ok = sem("xhi_ok")
        xlo_ok = sem("xlo_ok")
        gu_ps = sem("gu_ps")
        silu_ok = sem("silu_ok")
        h_ok = sem("h_ok")
        hT_ps = sem("hT_ps")
        hhi_ok = sem("hhi_ok")
        hlo_ok = sem("hlo_ok")
        y_ps = sem("y_ps")
        y_ok = sem("y_ok")
        y_out = [sem(f"y_out{n}") for n in range(TPE)]

        block = ctx.enter_context(nc.Block())

        x_t = x.rearrange("(j p) h -> p j h", p=P)
        xf_t = xf_dram.rearrange("(j p) h -> p j h", p=P)
        out_t = out[0:N, :].rearrange("(j p) h -> p j h", p=P)

        def over_tokens(eng, step):
            for s in range(XR):
                step(s, s)
            with eng.Fori(1, TT // XR) as i:
                for s in range(XR):
                    step(i * XR + s, s)

        def over_slots(eng, step):
            for s in range(FIRST):
                step(0, s)
            with eng.Fori(0, PASSES) as i:
                for s in range(FIRST, FIRST + PASS):
                    step(i, s)
            for s in range(FIRST, NT - PASS * PASSES):
                step(PASSES, s)

        def tile(i, s):
            return i * PASS + s

        def expert(i, s):
            return i * (PASS // TPE) + s // TPE

        def known(i, s):
            return i * PASS + s if isinstance(i, int) else FIRST

        @block.sync
        def _(sp):
            for half in range(2):
                sp.dma_start(condb[half * C:(half + 1) * C, :],
                             cond[half:half + 1, :].broadcast_to([C, TT])).then_inc(cond_in, 16)
            sp.dma_start(wr_sb[:, :, :], wr.rearrange("(k p) e -> p k e", p=P)).then_inc(wr_in, 16)

            def load_x(n, s):
                if not isinstance(n, int):
                    sp.wait_ge(x_in[s], (n - s) // XR * 16)
                sp.dma_start(x_sb[:, bass.ds(n, 1), :], x_t[:, bass.ds(n, 1), :]).then_inc(x_in[s], 16)

            over_tokens(sp, load_x)

            def load_unit(e, u):
                a, b = UNIT[u]
                if u < KH:
                    for w, o in ((wg, a), (wu, a + I)):
                        sp.dma_start(raw[:, o:o + I], w[bass.ds(e, 1), u * P:(u + 1) * P, :]
                                     .rearrange("o p i -> (o p) i")).then_inc(raw_in[u], 16)
                else:
                    full = (KI - 1) * P
                    sp.dma_start(raw[:, a:a + (KI - 1) * H].rearrange("p (c h) -> p c h", c=KI - 1),
                                 wd[bass.ds(e, 1), 0:full, :]
                                 .rearrange("o (c p) h -> p (o c) h", p=P)).then_inc(raw_in[u], 16)
                    sp.dma_start(raw[0:IR, a + (KI - 1) * H:b], wd[bass.ds(e, 1), full:I, :]
                                 .rearrange("o p h -> (o p) h")).then_inc(raw_in[u], 16)

            sp.wait_ge(pad_ok, 1)
            for u in range(NU):
                load_unit(0, u)
            def store_xf(n, s):
                sp.wait_ge(xf_ok, n + 1)
                sp.dma_start(xf_t[:, bass.ds(n, 1), :], xf_sb[:, s:s + 1, :]).then_inc(xf_out[s], 16)

            over_tokens(sp, store_xf)
            for u in range(NU):
                sp.wait_ge(wlo0_ok, u + 1)
                load_unit(1, u)
            sp.wait_ge(zeros_ok, 1)
            for s in range(XR):
                sp.wait_ge(x_in[s], 16 * (TT // XR))
            for q in range(TT // XR):
                sp.dma_start(out_t[:, q * XR:(q + 1) * XR, :],
                             x_sb[:, q * XR:(q + 1) * XR, :]).then_inc(out_init, 16)
            for t in range(TPE):
                sp.dma_start(out[N + t * P:N + (t + 1) * P, :], zeros[:, :]).then_inc(out_init, 16)
            with sp.Fori(2, E) as e:
                for u in range(NU):
                    sp.wait_ge(wlo_ok, (e - 2) * NU + u + 1)
                    load_unit(e, u)

        @block.gpsimd
        def _(pool):
            for half in range(2):
                nc.gpsimd.iota(row_in_c[half * C:(half + 1) * C, :], [[0, 1]], base=0,
                               channel_multiplier=1,
                               allow_small_or_imprecise_dtypes=True).then_inc(consts, 1)
                pool.wait_ge(consts, half + 1)
            nc.gpsimd.memset(raw[96:P, DOWN + (KI - 1) * H:WC], 0.0).then_inc(pad_ok, 1)
            pool.wait_ge(pad_ok, 1)
            nc.gpsimd.memset(wbd[:, :, :], 0.0).then_inc(consts, 1)
            pool.wait_ge(cidx_ok, 1)
            for j in range(TT):
                if j >= XR:
                    pool.wait_ge(wc_in[j % XR], 16 * (j // XR))
                nc.gpsimd.indirect_dma_start(
                    out=wc_sb[:, j, :], out_offset=None, in_=wcond[:, :],
                    in_offset=bass.IndirectOffsetOnAxis(ap=cidx[:, j:j + 1], axis=0),
                ).then_inc(wc_in[j % XR], 16)
            nc.gpsimd.memset(ident[:, :], 0.0).then_inc(consts, 1)
            nc.gpsimd.memset(upper[:, :], 1.0).then_inc(consts, 1)
            nc.gpsimd.memset(carry[:, :, :], 1.0).then_inc(consts, 1)
            pool.wait_ge(consts, 6)
            nc.gpsimd.affine_select(out=ident[:, :], in_=ident[:, :], compare_op=ALU.not_equal,
                                    fill=1.0, base=0, pattern=[[-1, P]],
                                    channel_multiplier=1).then_inc(consts, 1)
            nc.gpsimd.affine_select(out=upper[:, :], in_=upper[:, :], compare_op=ALU.is_ge,
                                    fill=0.0, base=0, pattern=[[1, P]],
                                    channel_multiplier=-1).then_inc(consts, 1)
            nc.gpsimd.memset(carry[:, :, 0:1], 0.0).then_inc(consts, 1)
            nc.gpsimd.memset(ones[:, :], 1.0).then_inc(consts, 1)
            nc.gpsimd.memset(zeros[:, :], 0.0).then_inc(zeros_ok, 1)
            nc.gpsimd.memset(h_sb[:, I:IP], 0.0).then_inc(consts, 1)
            for t, pattern, base, step in (
                    (iota_e[:, :], [[1, E]], 0, 0), (iota_p[:, :], [[1, P]], 0, 0),
                    (iota_t[:, :], [[1, NT]], 0, 0), (token1[:, :], [[P, TT]], 1, 1),
                    (spare[:, :], [[0, E], [P, TPE]], N + 1, 1)):
                nc.gpsimd.iota(t, pattern, base=base, channel_multiplier=step,
                               allow_small_or_imprecise_dtypes=True).then_inc(consts, 1)

            for u, (a, b) in enumerate(UNIT):
                pool.wait_ge(whi_ok, u + 1)
                nc.gpsimd.tensor_tensor(wlo[:, 0, a:b], raw[:, a:b], whi[:, 0, a:b].bitcast(F32),
                                        ALU.subtract).then_inc(wlo0_ok, 1)

            pool.wait_ge(lists_ok, 3)
            for s in range(XR):
                pool.wait_ge(xf_out[s], 16 * (TT // XR))

            def gather(n):
                if n >= TPE:
                    pool.wait_ge(xT_ps, n - TPE + 1)
                nc.gpsimd.indirect_dma_start(
                    out=xg[:, n % TPE, :], out_offset=None, in_=xf_dram[:, :],
                    in_offset=bass.IndirectOffsetOnAxis(ap=src_row[:, n:n + 1], axis=0),
                ).then_inc(xg_in[n % TPE], 16)

            def scatter(n):
                if n % TPE == 0 and n > 0:
                    for q in range(TPE):
                        pool.wait_ge(y_out[q], 16 * (n // TPE))
                pool.wait_ge(y_ok, n + 1)
                nc.gpsimd.indirect_dma_start(
                    out=out[:, :], in_=y_sb[:, n % TPE, :], in_offset=None,
                    out_offset=bass.IndirectOffsetOnAxis(ap=dst_row[:, n:n + 1], axis=0),
                    compute_op=ALU.add,
                ).then_inc(y_out[n % TPE], 16)

            AHEAD = 4
            for n in range(AHEAD):
                gather(n)
            pool.wait_ge(out_init, 16 * (TT // XR + TPE))
            for n in range(NT):
                if n + AHEAD < NT:
                    gather(n + AHEAD)
                scatter(n)
            for t in range(TPE):
                pool.wait_ge(y_out[t], 16 * E)

        @block.scalar
        def _(act):
            def xf_copy(n, s):
                act.wait_ge(xf_ps, n + 1)
                if not isinstance(n, int):
                    act.wait_ge(xf_out[s], (n - s) // XR * 16)
                    act.wait_ge(t_ps, n - XR + 1)
                nc.scalar.activation(xf_sb[:, s, :], ps_xf[s % 2][:, :], ACT.Copy).then_inc(xf_ok, 1)

            over_tokens(act, xf_copy)
            act.wait_ge(sub_ok, 1)
            nc.scalar.activation(ex[:, :, :], lg[:, :, :], ACT.Exp).then_inc(ex_ok, 1)

            def w_high(u, e_in_pair, count):
                a, b = UNIT[u]
                act.wait_ge(raw_in[u], count)
                nc.scalar.activation(whi[:, e_in_pair, a:b], raw[:, a:b], ACT.Copy).then_inc(whi_ok, 1)

            for u in range(NU):
                w_high(u, 0, 32)

            def x_high(i, s):
                act.wait_ge(xT_ps, tile(i, s) + 1)
                nc.scalar.activation(xhi[:, s % 2, :], ps_xT[:, :], ACT.Copy).then_inc(xhi_ok, 1)

            def y_scale(i, s):
                act.wait_ge(y_ps, tile(i, s) + 1)
                if known(i, s) >= TPE:
                    act.wait_ge(y_out[s % TPE], expert(i, s) * 16)
                nc.scalar.activation(y_sb[:, s % TPE, :], ps_y[:, :], ACT.Copy,
                                     scale=w_slot[:, bass.ds(tile(i, s), 1)]).then_inc(y_ok, 1)

            def step(i, s):
                if known(i, s) < NT - 1:
                    x_high(i, s + 1)
                act.wait_ge(gu_ps, tile(i, s) + 1)
                nc.scalar.activation(g_sb[:, :], ps_gate[:, 0:I], ACT.Silu).then_inc(silu_ok, 1)
                if 1 <= known(i, s) <= NT - TPE:
                    w_high((s - 1) % NU, ((s - 1) // NU + 1) % 2, (expert(i, s - 1) + 2) * 32)
                if known(i, s) > 0:
                    y_scale(i, s - 1)
                act.wait_ge(hT_ps, tile(i, s) + 1)
                nc.scalar.activation(hhi[:, :], ps_hT[:, 0:IP], ACT.Copy).then_inc(hhi_ok, 1)

            act.wait_ge(lists_ok, 3)
            x_high(0, 0)
            over_slots(act, step)
            y_scale(PASSES, NT - 1 - PASS * PASSES)

        @block.vector
        def _(dve):
            dve.wait_ge(cond_in, 32)
            dve.wait_ge(consts, 3)
            nc.vector.tensor_scalar(cidx[:, :], condb[:, :], float(C), row_in_c[:, :], ALU.mult,
                                    ALU.add).then_inc(cidx_ok, 1)

            def diagonal(n, s):
                if not isinstance(n, int):
                    dve.wait_ge(xf_ps, n - XR + 1)
                dve.wait_ge(wc_in[s], ((n - s) // XR + 1) * 16)
                for half in range(2):
                    rows = slice(half * C, (half + 1) * C)
                    nc.vector.tensor_copy(wbd[rows, s, half * D:(half + 1) * D],
                                          wc_sb[rows, bass.ds(n, 1), :]
                                          .rearrange("p o d -> p (o d)")).then_inc(wbd_ok, 1)

            def xfT_copy(n, s):
                dve.wait_ge(t_ps, n + 1)
                if not isinstance(n, int) or n >= 2:
                    dve.wait_ge(lg_ps, n - 1)
                nc.vector.tensor_copy(xfT[:, s % 2, :], ps_t[s % 2][:, :]).then_inc(xfT_ok, 1)

            def token_step(n, s):
                diagonal(n, s)
                if not isinstance(n, int) or n >= 2:
                    xfT_copy(n - 2, (s - 2) % XR)

            over_tokens(dve, token_step)
            for n in range(TT - 2, TT):
                xfT_copy(n, n % XR)

            chain = [0]

            def link(ins):
                chain[0] += 1
                ins.then_inc(route, 1)
                dve.wait_ge(route, chain[0])

            dve.wait_ge(consts, 16)
            dve.wait_ge(lg_ps, TT)
            lg_v = ps_lg[:, 0:TT * E].rearrange("p (j e) -> p j e", e=E)
            link(nc.vector.reduce_max(mx[:, :], lg_v, AX))
            nc.vector.tensor_tensor(lg[:, :, :], lg_v, mx[:, :].unsqueeze(2).broadcast_to([P, TT, E]),
                                    ALU.subtract).then_inc(sub_ok, 1)
            dve.wait_ge(ex_ok, 1)
            link(nc.vector.reduce_sum(sm[:, :], ex[:, :, :], AX))
            link(nc.vector.reciprocal(sm[:, :], sm[:, :]))
            link(nc.vector.tensor_tensor(gate[:, :, :], ex[:, :, :],
                                         sm[:, :].unsqueeze(2).broadcast_to([P, TT, E]), ALU.mult))
            for j in range(TT):
                last = nc.vector.max(v8[:, j, :], gate[:, j, :])
            link(last)
            for j in range(TT):
                last = nc.vector.max_index(i8[:, j, :], v8[:, j, :], gate[:, j, :])
            link(last)
            nc.vector.tensor_copy(choice[:, :, :], i8[:, :, 0:TOP].rearrange("p j c -> p c j"))
            nc.vector.tensor_copy(val[:, :, :], v8[:, :, 0:TOP].rearrange("p j c -> p c j"))
            link(nc.vector.tensor_copy(tok1[:, :, :],
                                       token1[:, :].unsqueeze(1).broadcast_to([P, TOP, TT])))
            ch = choice[:, :, :].rearrange("p c j -> p (c j)")
            nc.vector.tensor_tensor(oh[:, :, :], iota_e[:, :].unsqueeze(2).broadcast_to([P, E, A]),
                                    ch.unsqueeze(1).broadcast_to([P, E, A]),
                                    ALU.is_equal).then_inc(oh_ok, 1)
            dve.wait_ge(rank_ps, 1)
            EA = E * A
            within, total = ps_rank[:, 0:EA], ps_rank[:, EA:2 * EA]

            def flat(t):
                return t[:, :, :].rearrange("p e a -> p (e a)")

            link(nc.vector.tensor_tensor_scan(flat(run), flat(carry), total, 0.0, ALU.mult, ALU.add))
            link(nc.vector.tensor_tensor(flat(run), flat(run), total, ALU.subtract))
            link(nc.vector.tensor_tensor(flat(rk), flat(run), within, ALU.add))
            link(nc.vector.tensor_tensor(flat(rk), flat(rk), flat(oh), ALU.mult))
            link(nc.vector.reduce_sum(r1[:, :], rk[:, :, :].rearrange("p e a -> p a e"), AX))
            nc.vector.tensor_scalar(over[:, :], r1[:, :], float(CAP), float(FAR), ALU.is_gt, ALU.mult)
            link(nc.vector.scalar_tensor_tensor(slot_f[:, :], ch, float(CAP), r1[:, :], ALU.mult, ALU.add))
            link(nc.vector.scalar_tensor_tensor(slot[:, :], over[:, :], -1.0, slot_f[:, :], ALU.add, ALU.add))
            nc.vector.tensor_scalar(slot_i[:, 0, :], slot[:, :], 7, None, ALU.arith_shift_right)
            link(nc.vector.tensor_scalar(slot_i[:, 1, :], slot[:, :], P - 1, None, ALU.bitwise_and))
            link(nc.vector.tensor_copy(slot_tp[:, :, :], slot_i[:, :, :]))
            link(nc.vector.tensor_tensor(pick_t[:, :, :], iota_t[:, :].unsqueeze(1).broadcast_to([P, A, NT]),
                                         slot_tp[:, 0, :].unsqueeze(2).broadcast_to([P, A, NT]), ALU.is_equal))
            for q, v in enumerate((tok1, val)):
                vv = v[:, :, :].rearrange("p c j -> p (c j)").unsqueeze(2).broadcast_to([P, A, NT])
                nc.vector.tensor_tensor(what[:, :, q * NT:(q + 1) * NT], pick_t[:, :, :], vv, ALU.mult)
            for q in range(4):
                a = slice(q * A // 4, (q + 1) * A // 4)
                nc.vector.tensor_tensor(
                    pick_p[:, a, :], iota_p[:, :].unsqueeze(1).broadcast_to([P, A // 4, P]),
                    slot_tp[:, 1, a].unsqueeze(2).broadcast_to([P, A // 4, P]),
                    ALU.is_equal).then_inc(pick_ok, 1)
            dve.wait_ge(slot_ps, 1)
            got, gates = ps_slot[:, 0:NT], ps_slot[:, NT:2 * NT]
            nc.vector.tensor_scalar(src_row[:, :], got, -1.0, 0.0, ALU.add, ALU.max).then_inc(lists_ok, 1)
            link(nc.vector.scalar_tensor_tensor(empty[:, :], got, 0.0, spare[:, :], ALU.is_equal, ALU.mult))
            nc.vector.scalar_tensor_tensor(dst_row[:, :], got, -1.0, empty[:, :], ALU.add,
                                           ALU.add).then_inc(lists_ok, 1)
            nc.vector.tensor_copy(w_slot[:, :], gates).then_inc(lists_ok, 1)

            def x_low(i, s):
                dve.wait_ge(xhi_ok, tile(i, s) + 1)
                nc.vector.tensor_tensor(xlo[:, s % 2, :], ps_xT[:, :], xhi[:, s % 2, :].bitcast(F32),
                                        ALU.subtract).then_inc(xlo_ok, 1)

            def step(i, s):
                if known(i, s) < NT - 1:
                    x_low(i, s + 1)
                dve.wait_ge(silu_ok, tile(i, s) + 1)
                nc.vector.tensor_tensor(h_sb[:, 0:I], g_sb[:, :], ps_up[:, 0:I], ALU.mult).then_inc(h_ok, 1)
                if 1 <= known(i, s) <= NT - TPE:
                    a, b = UNIT[(s - 1) % NU]
                    half = ((s - 1) // NU + 1) % 2
                    dve.wait_ge(whi_ok, tile(i, s) + NU)
                    nc.vector.tensor_tensor(wlo[:, half, a:b], raw[:, a:b], whi[:, half, a:b].bitcast(F32),
                                            ALU.subtract).then_inc(wlo_ok, 1)
                dve.wait_ge(hhi_ok, tile(i, s) + 1)
                nc.vector.tensor_tensor(hlo[:, :], ps_hT[:, 0:IP], hhi[:, :].bitcast(F32),
                                        ALU.subtract).then_inc(hlo_ok, 1)

            x_low(0, 0)
            over_slots(dve, step)

        @block.tensor
        def _(pe):
            def condition(n, s):
                pe.wait_ge(wbd_ok, (n + 1) * 2)
                pe.wait_ge(x_in[s], ((n - s) // XR + 1) * 16)
                if not isinstance(n, int) or n >= 2:
                    pe.wait_ge(xf_ok, n - 1)
                nc.tensor.matmul(ps_xf[s % 2][:, :], wbd[:, s, :],
                                 x_sb[:, bass.ds(n, 1), :].rearrange("p o h -> p (o h)"),
                                 start=True, stop=True).then_inc(xf_ps, 1)

            def turn(n, s):
                pe.wait_ge(xf_ok, n + 1)
                if not isinstance(n, int) or n >= 2:
                    pe.wait_ge(xfT_ok, n - 1)
                for k in range(KH):
                    last = nc.tensor.transpose(ps_t[s % 2][:, k * P:(k + 1) * P],
                                               xf_sb[:, s, k * P:(k + 1) * P], ident[:, :])
                last.then_inc(t_ps, 1)

            def logits(n, s):
                pe.wait_ge(xfT_ok, n + 1)
                for k in range(KH):
                    last = nc.tensor.matmul(ps_lg[:, bass.ds(n * E, E)], xfT[:, s % 2, k * P:(k + 1) * P],
                                            wr_sb[:, k, :], start=(k == 0), stop=(k == KH - 1))
                last.then_inc(lg_ps, 1)

            pe.wait_ge(consts, 16)
            pe.wait_ge(wr_in, 16)
            def token_step(n, s):
                condition(n, s)
                if not isinstance(n, int) or n >= 1:
                    turn(n - 1, (s - 1) % XR)
                if not isinstance(n, int) or n >= 2:
                    logits(n - 2, (s - 2) % XR)

            over_tokens(pe, token_step)
            turn(TT - 1, (TT - 1) % XR)
            for n in range(TT - 2, TT):
                logits(n, n % XR)

            pe.wait_ge(oh_ok, 1)
            o = oh[:, :, :].rearrange("p e a -> p (e a)")
            nc.tensor.matmul(ps_rank[:, 0:E * A], upper[:, :], o, start=True, stop=True)
            nc.tensor.matmul(ps_rank[:, E * A:2 * E * A], ones[:, :], o,
                             start=True, stop=True).then_inc(rank_ps, 1)
            for a in range(A):
                if a % (A // 4) == 0:
                    pe.wait_ge(pick_ok, a // (A // 4) + 1)
                last = nc.tensor.matmul(ps_slot[:, 0:2 * NT], pick_p[:, a, :], what[:, a, :],
                                        start=(a == 0), stop=(a == A - 1))
            last.then_inc(slot_ps, 1)

            def x_turn(i, s):
                pe.wait_ge(xg_in[s % TPE], (expert(i, s) + 1) * 16)
                if known(i, s) > 0:
                    pe.wait_ge(xlo_ok, tile(i, s))
                for k in range(KH):
                    last = nc.tensor.transpose(ps_xT[:, k * P:(k + 1) * P],
                                               xg[:, s % TPE, k * P:(k + 1) * P], ident[:, :])
                last.then_inc(xT_ps, 1)

            def gate_up(s, ks):
                half = (s // TPE) % 2
                for k in ks:
                    g, u = k * 2 * I, k * 2 * I + I
                    c = slice(k * P, (k + 1) * P)
                    for q, (left, right) in enumerate(((xhi, whi), (xhi, wlo), (xlo, whi))):
                        for ps, o in ((ps_gate, g), (ps_up, u)):
                            last = nc.tensor.matmul(ps[:, 0:I], left[:, s % 2, c], right[:, half, o:o + I],
                                                    start=(k == 0 and q == 0), stop=(k == KH - 1 and q == 2))
                if KH - 1 in ks:
                    last.then_inc(gu_ps, 1)

            def down(i, s):
                half = (s // TPE) % 2
                pe.wait_ge(hlo_ok, tile(i, s) + 1)
                if s % TPE == 0 and known(i, s) > 0:
                    pe.wait_ge(wlo_ok, tile(i, s))
                if known(i, s) > 0:
                    pe.wait_ge(y_ok, tile(i, s))
                for c in range(KI):
                    o = DOWN + c * H
                    for q, (left, right) in enumerate(((hhi, whi), (hhi, wlo), (hlo, whi))):
                        last = nc.tensor.matmul(ps_y[:, :], left[:, c * P:(c + 1) * P],
                                                right[:, half, o:o + H],
                                                start=(c == 0 and q == 0), stop=(c == KI - 1 and q == 2))
                last.then_inc(y_ps, 1)

            def step(i, s):
                pe.wait_ge(xlo_ok, tile(i, s) + 1)
                if known(i, s) == 0:
                    pe.wait_ge(wlo0_ok, NU)
                elif s % TPE == 0:
                    pe.wait_ge(wlo_ok, tile(i, s) - 1)
                gate_up(s, (0, 1))
                if known(i, s) < NT - 1:
                    x_turn(i, s + 1)
                gate_up(s, (2, 3))
                if known(i, s) > 0:
                    down(i, s - 1)
                pe.wait_ge(h_ok, tile(i, s) + 1)
                for c in range(KI):
                    last = nc.tensor.transpose(ps_hT[:, c * P:(c + 1) * P], h_sb[:, c * P:(c + 1) * P],
                                               ident[:, :])
                last.then_inc(hT_ps, 1)

            x_turn(0, 0)
            over_slots(pe, step)
            down(PASSES, NT - 1 - PASS * PASSES)


def kernel(x, itok_B_1_198, L0_cond_weights, L0_ffn_Wr, L0_ffn_Wg, L0_ffn_Wu, L0_ffn_Wd):
    import numpy as np
    import concourse.bacc as bacc
    from concourse.bass_utils import run_bass_kernel_spmd

    arrays = {
        "x": np.asarray(x).reshape(B * C, H),
        "cond": np.asarray(itok_B_1_198).reshape(TT, 2).T,
        "wcond": np.asarray(L0_cond_weights).reshape(S * C, D),
        "wr": np.asarray(L0_ffn_Wr).T,
        "wg": np.asarray(L0_ffn_Wg).transpose(0, 2, 1),
        "wu": np.asarray(L0_ffn_Wu).transpose(0, 2, 1),
        "wd": np.asarray(L0_ffn_Wd).transpose(0, 2, 1),
    }
    arrays = {name: np.ascontiguousarray(a) for name, a in arrays.items()}
    nc = bacc.Bacc("TRN2", target_bir_lowering=False, num_devices=1)
    ins = [nc.dram_tensor(name, a.shape, mybir.dt.from_np(a.dtype), kind="ExternalInput").ap()
           for name, a in arrays.items()]
    out = nc.dram_tensor("out", (N + CAP, H), F32, kind="ExternalOutput").ap()
    build(nc, *ins, out)
    r = run_bass_kernel_spmd(nc, [arrays], core_ids=[0])
    return r.results[0]["out"][0:N].reshape(B, C, H)
```

```python
from contextlib import ExitStack

import concourse.bass as bass
from concourse import mybir

B, C, D, H = 32, 64, 64, 512
N = B * D
S = 200
E, I = 8, 352
TOP = 2
CAP = int(1.25 * (N * TOP / E))
P = 128
Q = 32
TT = N // P
KH = H // P
KI = (I + P - 1) // P
IP = KI * P
IR = I - (KI - 1) * P
TPE = CAP // P
NT = E * TPE
A = TOP * TT
FAR = 100000

UNIT = [(k * 2 * I, (k + 1) * 2 * I) for k in range(KH)] + [(KH * 2 * I, KH * 2 * I + KI * H)]
NU = len(UNIT)
DOWN = UNIT[-1][0]
WC = UNIT[-1][1]

XR = 4
GR = 4
NG = TT // GR
HALF = TT // 2
QTY = 3
POOL_PICKS = 14

PASS = 2 * TPE
FIRST = TPE + 1
AHEAD = TPE
PASSES = (NT - FIRST) // PASS

F32 = mybir.dt.float32
F32R = mybir.dt.float32r
BF16 = mybir.dt.bfloat16
I32 = mybir.dt.int32
U32 = mybir.dt.uint32
U16 = mybir.dt.uint16
ALU = mybir.AluOpType
ACT = mybir.ActivationFunctionType
AX = mybir.AxisListType.X


def build(nc, x, xT, cond, wcond, wr, wg, wu, wd, out):
    xf_dram = nc.dram_tensor("xf_dram", (N, H), F32, kind="Internal").ap()
    ctx = ExitStack()
    with ctx:
        def sb(name, shape, dt=F32):
            return ctx.enter_context(nc.sbuf_tensor(name, shape, dt))

        def pb(name):
            return ctx.enter_context(nc.psum_tensor(name, [P, 512], F32))

        def sem(name):
            return ctx.enter_context(nc.semaphore(name))

        ident = sb("ident", [P, P])
        upper = sb("upper", [P, P], BF16)
        ones = sb("ones", [P, P], BF16)
        iota_e = sb("iota_e", [P, E])
        iota_p = sb("iota_p", [P, P])
        iota_t = sb("iota_t", [P, NT])
        row_in_c = sb("row_in_c", [P, 1])
        token1 = sb("token1", [P, TOP, TT])
        spare = sb("spare", [P, NT])
        carry = sb("carry", [P, E, A])
        zeros = sb("zeros", [P, H])

        condb = sb("condb", [P, TT], I32)
        cidx = sb("cidx", [P, TT], U32)
        wc_sb = sb("wc_sb", [P, TT, D])
        wbd = sb("wbd", [P, TT, 2 * D])
        wr_sb = sb("wr_sb", [P, KH, Q])
        x_sb = sb("x_sb", [P, TT, H])
        pick_t = sb("pick_t", [P, A, NT])
        xrT = sb("xrT", [P, NG, GR * P])
        xr = sb("xr", [P, TT, E])
        lg = sb("lg", [P, TT, E])
        mx = sb("mx", [P, TT])
        ex = sb("ex", [P, TT, E])
        sm = sb("sm", [P, TT])
        gate = sb("gate", [P, TT, E])
        v8 = sb("v8", [P, TT, 8])
        i8 = sb("i8", [P, TT, 8], U32)
        choice = sb("choice", [P, TOP, TT])
        val = sb("val", [P, TOP, TT])
        oh = sb("oh", [P, E, A], BF16)
        run = sb("run", [P, E, A])
        more = sb("more", [1, E], U16)
        rk = sb("rk", [P, E, A])
        r1 = sb("r1", [P, A])
        over = sb("over", [P, A])
        slot_f = sb("slot_f", [P, A])
        slot = sb("slot", [P, A], I32)
        slot_i = sb("slot_i", [P, 2, A], I32)
        slot_tp = sb("slot_tp", [P, 2, A])
        gate_hi = sb("gate_hi", [P, A], F32R)
        gate_lo = sb("gate_lo", [P, A], F32R)
        got = sb("got", [P, QTY, NT])
        empty = sb("empty", [P, NT])
        src_row = sb("src_row", [P, NT], U32)
        dst_row = sb("dst_row", [P, NT], U32)
        w_slot = sb("w_slot", [P, NT])

        raw = sb("raw", [P, WC])
        whi = sb("whi", [P, 2, WC], F32R)
        wlo = sb("wlo", [P, 2, WC], F32R)
        tiles = sb("tiles", [P, NG * KH * GR * P])
        xg = tiles[:, 0:TPE * H].rearrange("p (t h) -> p t h", h=H)
        y_sb = tiles[:, TPE * H:2 * TPE * H].rearrange("p (t h) -> p t h", h=H)
        xT_sb = tiles[:, :].rearrange("p (g k c) -> p g k c", g=NG, k=KH)
        xf_sb = tiles[:, :].rearrange("p (j h) -> p j h", h=H)
        pick_p = whi[:, 1, 0:A * P].rearrange("p (a q) -> p a q", q=P)
        what_tok = wlo[:, 1, 0:A * NT].rearrange("p (a t) -> p a t", t=NT)
        what_gate = wlo[:, 1, A * NT:3 * A * NT].rearrange("p (a v t) -> p a v t", v=2, t=NT)
        xhi = sb("xhi", [P, 3, H], F32R)
        xlo = sb("xlo", [P, 3, H], F32R)
        g_sb = sb("g_sb", [P, I])
        h_sb = sb("h_sb", [P, IP])
        hhi = sb("hhi", [P, IP], F32R)
        hlo = sb("hlo", [P, IP], F32R)

        bank = [pb(f"bank{n}") for n in range(8)]
        ps_xf = bank[0:XR]
        ps_xr, ps_lg = (bank[2], bank[3]), (bank[4], bank[7])
        ps_xrT = (bank[5], bank[6], bank[0], bank[1])
        ps_rank, ps_slot, ps_slot_gate = bank[5], bank[6], bank[7]
        ps_gate, ps_up, ps_hT, ps_xT, ps_y = bank[5], bank[6], bank[7], bank[2], bank[0]

        consts = sem("consts")
        CONSTS = 15
        cond_in = sem("cond_in")
        cidx_ok = sem("cidx_ok")
        wr_clear = sem("wr_clear")
        wr_in = sem("wr_in")
        zeros_ok = sem("zeros_ok")
        wc_in = [sem(f"wc_in{n}") for n in range(NG)]
        xT_in = [sem(f"xT_in{n}") for n in range(NG)]
        x_in = [sem(f"x_in{n}") for n in range(XR)]
        wbd_ok = sem("wbd_ok")
        wbd_last_ok = sem("wbd_last_ok")
        xf_ps = sem("xf_ps")
        xf_ok = sem("xf_ok")
        xf_out = sem("xf_out")
        xrT_ps = sem("xrT_ps")
        xrT_ok = sem("xrT_ok")
        xr_ps = sem("xr_ps")
        xr_ok = sem("xr_ok")
        lg_ps = sem("lg_ps")
        sub_ok = sem("sub_ok")
        ex_ok = sem("ex_ok")
        route = sem("route")
        oh_ok = sem("oh_ok")
        wbd_clear = sem("wbd_clear")
        rank_ps = sem("rank_ps")
        more_ok = sem("more_ok")
        slot_ok = sem("slot_ok")
        pool_pick_ok = sem("pool_pick_ok")
        pick_ok = sem("pick_ok")
        gate_pick_ok = sem("gate_pick_ok")
        slot_ps = sem("slot_ps")
        slot_gates_ps = sem("slot_gates_ps")
        w_slot_ok = sem("w_slot_ok")
        lists_ok = sem("lists_ok")
        out_init = sem("out_init")
        raw_in = [sem(f"raw_in{u}") for u in range(NU)]
        pad_ok = sem("pad_ok")
        whi_ok = sem("whi_ok")
        wlo0_ok = sem("wlo0_ok")
        wlo_ok = sem("wlo_ok")
        xg_in = [sem(f"xg_in{n}") for n in range(TPE)]
        xT_ps = sem("xT_ps")
        xhi_ok = sem("xhi_ok")
        xlo_ok = sem("xlo_ok")
        gu_ps = sem("gu_ps")
        silu_warm = sem("silu_warm")
        silu_ok = sem("silu_ok")
        h_ok = sem("h_ok")
        hT_ps = sem("hT_ps")
        hhi_ok = sem("hhi_ok")
        hlo_ok = sem("hlo_ok")
        y_ps = sem("y_ps")
        y_ok = sem("y_ok")
        y_out = [sem(f"y_out{n}") for n in range(TPE)]

        block = ctx.enter_context(nc.Block())

        x_t = x.rearrange("(j p) h -> p j h", p=P)
        xf_t = xf_dram.rearrange("(j p) h -> p j h", p=P)
        out_t = out[0:N, :].rearrange("(j p) h -> p j h", p=P)

        def over_tokens(eng, step):
            for s in range(XR):
                step(s, s)
            with eng.Fori(1, TT // XR) as i:
                for s in range(XR):
                    step(i * XR + s, s)

        def passed_over(eng, i, s, full, short):
            more_there = eng.value_load(more[0:1, bass.ds(expert(i, s), 1)])
            with eng.If(more_there > 0):
                full()
            with eng.Else():
                short()

        def over_slots(eng, step):
            def steps(i, s):
                if s % TPE < TPE - 2:
                    step(i, s, 1)
                elif s % TPE == TPE - 2:
                    def both():
                        step(i, s, 1)
                        step(i, s + 1, 1)

                    passed_over(eng, i, s, both, lambda: step(i, s, 2))

            for s in range(FIRST):
                steps(0, s)
            with eng.Fori(0, PASSES) as i:
                for s in range(FIRST, FIRST + PASS):
                    steps(i, s)
            for s in range(FIRST, NT - PASS * PASSES):
                steps(PASSES, s)

        def tile_before(eng, i, s, do):
            if s % TPE == 0:
                passed_over(eng, i, s - 1, lambda: do(i, s - 1, 1), lambda: do(i, s - 2, 2))
            else:
                do(i, s - 1, 1)

        def tile(i, s):
            return i * PASS + s

        def expert(i, s):
            return i * (PASS // TPE) + s // TPE

        def half_of(s):
            return (s // TPE) % 2

        def x_buffer(s):
            return 2 if s % TPE == TPE - 1 else s % TPE % 2

        def known(i, s):
            return i * PASS + s if isinstance(i, int) else FIRST

        @block.sync
        def _(sp):
            for half in range(2):
                sp.dma_start(condb[half * C:(half + 1) * C, :],
                             cond[half:half + 1, :].broadcast_to([C, TT])).then_inc(cond_in, 16)
            xT_v = xT.rearrange("(k p) c -> p k c", p=P)

            def load_xT(g):
                sp.dma_start(xT_sb[:, g, :, :],
                             xT_v[:, :, g * GR * P:(g + 1) * GR * P]).then_inc(xT_in[g], 16)

            load_xT(0)
            sp.wait_ge(wr_clear, 1)
            sp.dma_start(wr_sb[:, :, 0:E], wr.rearrange("(k p) e -> p k e", p=P)).then_inc(wr_in, 16)
            for g in range(1, NG):
                load_xT(g)

            def load_x(n, s):
                if not isinstance(n, int):
                    sp.wait_ge(x_in[s], (n - s) // XR * 16)
                sp.dma_start(x_sb[:, bass.ds(n, 1), :], x_t[:, bass.ds(n, 1), :]).then_inc(x_in[s], 16)


            def load_unit(e, u):
                a, b = UNIT[u]
                if u < KH:
                    for w, o in ((wg, a), (wu, a + I)):
                        sp.dma_start(raw[:, o:o + I], w[bass.ds(e, 1), u * P:(u + 1) * P, :]
                                     .rearrange("o p i -> (o p) i")).then_inc(raw_in[u], 16)
                else:
                    full = (KI - 1) * P
                    sp.dma_start(raw[:, a:a + (KI - 1) * H].rearrange("p (c h) -> p c h", c=KI - 1),
                                 wd[bass.ds(e, 1), 0:full, :]
                                 .rearrange("o (c p) h -> p (o c) h", p=P)).then_inc(raw_in[u], 16)
                    sp.dma_start(raw[0:IR, a + (KI - 1) * H:b], wd[bass.ds(e, 1), full:I, :]
                                 .rearrange("o p h -> (o p) h")).then_inc(raw_in[u], 16)

            over_tokens(sp, load_x)
            sp.wait_ge(pad_ok, 1)
            for u in range(NU):
                load_unit(0, u)
            with sp.Fori(0, TT // 2) as m:
                sp.wait_ge(xf_ok, m * 2 + 2)
                sp.dma_start(xf_t[:, bass.ds(m * 2, 2), :],
                             xf_sb[:, bass.ds(m * 2, 2), :]).then_inc(xf_out, 16)
            for u in range(NU):
                sp.wait_ge(wlo0_ok, u + 1)
                load_unit(1, u)
            for t in range(AHEAD):
                sp.wait_ge(xg_in[t], 16)
            sp.wait_ge(zeros_ok, 1)
            for s in range(XR):
                sp.wait_ge(x_in[s], 16 * (TT // XR))
            for q in range(TT // XR):
                sp.dma_start(out_t[:, q * XR:(q + 1) * XR, :],
                             x_sb[:, q * XR:(q + 1) * XR, :]).then_inc(out_init, 16)
            for t in range(TPE):
                sp.dma_start(out[N + t * P:N + (t + 1) * P, :], zeros[:, :]).then_inc(out_init, 16)
            with sp.Fori(2, E) as e:
                for u in range(NU):
                    sp.wait_ge(wlo_ok, (e - 2) * NU + u + 1)
                    load_unit(e, u)

        @block.gpsimd
        def _(pool):
            for half in range(2):
                nc.gpsimd.iota(row_in_c[half * C:(half + 1) * C, :], [[0, 1]], base=0,
                               channel_multiplier=1,
                               allow_small_or_imprecise_dtypes=True).then_inc(consts, 1)
                pool.wait_ge(consts, half + 1)
            nc.gpsimd.memset(raw[96:P, DOWN + (KI - 1) * H:WC], 0.0).then_inc(pad_ok, 1)
            pool.wait_ge(pad_ok, 1)
            nc.gpsimd.memset(ident[:, :], 0.0).then_inc(consts, 1)
            pool.wait_ge(consts, 3)
            nc.gpsimd.affine_select(out=ident[:, :], in_=ident[:, :], compare_op=ALU.not_equal,
                                    fill=1.0, base=0, pattern=[[-1, P]],
                                    channel_multiplier=1).then_inc(consts, 1)
            pool.wait_ge(cidx_ok, 1)
            for j in range(TT):
                nc.gpsimd.indirect_dma_start(
                    out=wc_sb[:, j, :], out_offset=None, in_=wcond[:, :],
                    in_offset=bass.IndirectOffsetOnAxis(ap=cidx[:, j:j + 1], axis=0),
                ).then_inc(wc_in[j // GR], 16)

            nc.gpsimd.memset(upper[:, :], 1.0).then_inc(consts, 1)
            nc.gpsimd.memset(carry[:, :, :], 1.0).then_inc(consts, 1)
            pool.wait_ge(consts, 6)
            nc.gpsimd.affine_select(out=upper[:, :], in_=upper[:, :], compare_op=ALU.is_ge,
                                    fill=0.0, base=0, pattern=[[1, P]],
                                    channel_multiplier=-1).then_inc(consts, 1)
            nc.gpsimd.memset(carry[:, :, 0:1], 0.0).then_inc(consts, 1)
            nc.gpsimd.memset(ones[:, :], 1.0).then_inc(consts, 1)
            nc.gpsimd.memset(zeros[:, :], 0.0).then_inc(zeros_ok, 1)
            nc.gpsimd.memset(h_sb[:, I:IP], 0.0).then_inc(consts, 1)
            for t, pattern, base, step in (
                    (iota_e[:, :], [[1, E]], 0, 0), (iota_p[:, :], [[1, P]], 0, 0),
                    (iota_t[:, :], [[1, NT]], 0, 0), (token1[:, :, :], [[0, TOP], [P, TT]], 1, 1),
                    (spare[:, :], [[0, E], [P, TPE]], N + 1, 1)):
                nc.gpsimd.iota(t, pattern, base=base, channel_multiplier=step,
                               allow_small_or_imprecise_dtypes=True).then_inc(consts, 1)

            pool.wait_ge(slot_ok, 1)
            for n in range(A - POOL_PICKS, A):
                nc.gpsimd.tensor_scalar(pick_p[:, n, :], iota_p[:, :], slot_tp[:, 1, n:n + 1], None,
                                        ALU.is_equal).then_inc(pool_pick_ok, 1)

            pool.wait_ge(lists_ok, 1)
            pool.wait_ge(xf_out, 16 * (TT // 2))

            def gather(n):
                if n >= TPE:
                    pool.wait_ge(xT_ps, n - TPE + 1)
                nc.gpsimd.indirect_dma_start(
                    out=xg[:, n % TPE, :], out_offset=None, in_=xf_dram[:, :],
                    in_offset=bass.IndirectOffsetOnAxis(ap=src_row[:, n:n + 1], axis=0),
                ).then_inc(xg_in[n % TPE], 16)

            def scatter(n):
                if n % TPE == 0 and n > 0:
                    for q in range(TPE):
                        pool.wait_ge(y_out[q], 16 * (n // TPE))
                pool.wait_ge(y_ok, n + 1)
                nc.gpsimd.indirect_dma_start(
                    out=out[:, :], in_=y_sb[:, n % TPE, :], in_offset=None,
                    out_offset=bass.IndirectOffsetOnAxis(ap=dst_row[:, n:n + 1], axis=0),
                    compute_op=ALU.add,
                ).then_inc(y_out[n % TPE], 16)

            for n in range(AHEAD):
                gather(n)
            pool.wait_ge(out_init, 16 * (TT // XR + TPE))
            pool.wait_ge(lists_ok, 2)
            for n in range(NT):
                if n + AHEAD < NT:
                    gather(n + AHEAD)
                scatter(n)
            for t in range(TPE):
                pool.wait_ge(y_out[t], 16 * E)

        @block.scalar
        def _(act):
            def exps(h):
                act.wait_ge(sub_ok, h + 1)
                js = slice(h * HALF, (h + 1) * HALF)
                nc.scalar.activation(ex[:, js, :], lg[:, js, :], ACT.Exp).then_inc(ex_ok, 1)

            def xf_copy(n, s):
                act.wait_ge(xf_ps, n + 1)
                nc.scalar.activation(xf_sb[:, bass.ds(n, 1), :], ps_xf[s][:, :].unsqueeze(1),
                                     ACT.Copy).then_inc(xf_ok, 1)

            exps(0)
            js = slice((NG - 1) * GR, TT)
            act.wait_ge(wbd_clear, 1)
            act.wait_ge(wc_in[NG - 1], 16 * GR)
            for half in range(2):
                rows = slice(half * C, (half + 1) * C)
                nc.scalar.activation(wbd[rows, js, half * D:(half + 1) * D], wc_sb[rows, js, :],
                                     ACT.Copy).then_inc(wbd_last_ok, 1)
            xf_copy(0, 0)
            exps(1)
            for n in range(1, XR):
                xf_copy(n, n)
            with act.Fori(1, TT // XR) as i:
                for s in range(XR):
                    xf_copy(i * XR + s, s)

            def w_high(u, e_in_pair, count):
                a, b = UNIT[u]
                act.wait_ge(raw_in[u], count)
                nc.scalar.activation(whi[:, e_in_pair, a:b], raw[:, a:b], ACT.Copy).then_inc(whi_ok, 1)

            for u in range(NU):
                w_high(u, 0, 32)

            def x_high(i, s, n):
                act.wait_ge(xT_ps, tile(i, s) + 1)
                nc.scalar.activation(xhi[:, x_buffer(s), :], ps_xT[:, :], ACT.Copy).then_inc(xhi_ok, n)

            def next_w_high(i, s):
                if 1 <= known(i, s) <= NT - TPE:
                    w_high((s - 1) % NU, ((s - 1) // NU + 1) % 2, (expert(i, s - 1) + 2) * 32)

            def y_scale(i, s, n):
                act.wait_ge(y_ps, tile(i, s) + 1)
                if known(i, s) >= TPE:
                    act.wait_ge(y_out[s % TPE], expert(i, s) * 16)
                elif known(i, s) == 0:
                    act.wait_ge(w_slot_ok, 1)
                nc.scalar.activation(y_sb[:, s % TPE, :], ps_y[:, :], ACT.Copy,
                                     scale=w_slot[:, bass.ds(tile(i, s), 1)]).then_inc(y_ok, n)

            def step(i, s, n):
                if known(i, s) + n < NT:
                    x_high(i, s + n, n)
                act.wait_ge(gu_ps, tile(i, s) + 1)
                nc.scalar.activation(g_sb[:, :], ps_gate[:, 0:I], ACT.Silu).then_inc(silu_ok, n)
                for t in range(s, s + n):
                    next_w_high(i, t)
                if known(i, s) > 0:
                    tile_before(act, i, s, y_scale)
                act.wait_ge(hT_ps, tile(i, s) + 1)
                nc.scalar.activation(hhi[:, :], ps_hT[:, 0:IP], ACT.Copy).then_inc(hhi_ok, n)

            act.wait_ge(zeros_ok, 1)
            nc.scalar.activation(g_sb[:, 0:1], zeros[:, 0:1], ACT.Silu).then_inc(silu_warm, 1)
            x_high(0, 0, 1)
            act.wait_ge(silu_warm, 1)
            act.wait_ge(more_ok, 1)
            over_slots(act, step)
            tile_before(act, PASSES, NT - PASS * PASSES, y_scale)

        @block.vector
        def _(dve):
            nc.vector.memset(wr_sb[:, :, :], 0.0).then_inc(wr_clear, 1)
            dve.wait_ge(cond_in, 32)
            dve.wait_ge(consts, 2)
            nc.vector.tensor_scalar(cidx[:, :], condb[:, :], float(C), row_in_c[:, :], ALU.mult,
                                    ALU.add).then_inc(cidx_ok, 1)

            nc.vector.memset(wbd[:, :, :], 0.0).then_inc(wbd_clear, 1)
            dve.wait_ge(wbd_clear, 1)

            def diagonal(g):
                js = slice(g * GR, (g + 1) * GR)
                dve.wait_ge(wc_in[g], 16 * GR)
                for half in range(2):
                    rows = slice(half * C, (half + 1) * C)
                    nc.vector.tensor_copy(wbd[rows, js, half * D:(half + 1) * D],
                                          wc_sb[rows, js, :]).then_inc(wbd_ok, 1)

            chain = [0]

            def link(ins):
                chain[0] += 1
                ins.then_inc(route, 1)
                dve.wait_ge(route, chain[0])

            def gates(h):
                js = slice(h * HALF, (h + 1) * HALF)
                wide = [P, HALF, E]
                dve.wait_ge(lg_ps, (h + 1) * (NG // 2))
                lg_v = ps_lg[h][:, 0:HALF * E].rearrange("p (j e) -> p j e", e=E)
                link(nc.vector.reduce_max(mx[:, js], lg_v, AX))
                nc.vector.tensor_tensor(lg[:, js, :], lg_v, mx[:, js].unsqueeze(2).broadcast_to(wide),
                                        ALU.subtract).then_inc(sub_ok, 1)
                dve.wait_ge(ex_ok, h + 1)
                link(nc.vector.reduce_sum(sm[:, js], ex[:, js, :], AX))
                link(nc.vector.reciprocal(sm[:, js], sm[:, js]))
                link(nc.vector.tensor_tensor(gate[:, js, :], ex[:, js, :],
                                             sm[:, js].unsqueeze(2).broadcast_to(wide), ALU.mult))
                for j in range(h * HALF, (h + 1) * HALF):
                    last = nc.vector.max(v8[:, j, :], gate[:, j, :])
                link(last)
                for j in range(h * HALF, (h + 1) * HALF):
                    last = nc.vector.max_index(i8[:, j, :], v8[:, j, :], gate[:, j, :])
                link(last)

            def xrT_copy(g):
                dve.wait_ge(xrT_ps, g + 1)
                nc.vector.tensor_copy(xrT[:, g, :], ps_xrT[g][:, :]).then_inc(xrT_ok, 1)

            def xr_sum(g):
                dve.wait_ge(xr_ps, g + 1)
                js = slice(g * GR, (g + 1) * GR)
                nc.vector.reduce_sum(xr[:, js, :], ps_xr[g % 2][:, :]
                                     .rearrange("p (j k c) -> p j c k", j=GR, k=KH)[:, :, 0:E, :],
                                     AX).then_inc(xr_ok, 1)

            for g in range(NG + 1):
                if g < NG:
                    xrT_copy(g)
                if g >= 1:
                    xr_sum(g - 1)
            for g in range(NG - 1):
                diagonal(g)
            for h in range(2):
                gates(h)
            dve.wait_ge(consts, CONSTS)
            nc.vector.tensor_copy(choice[:, :, :], i8[:, :, 0:TOP].rearrange("p j c -> p c j"))
            link(nc.vector.tensor_copy(val[:, :, :], v8[:, :, 0:TOP].rearrange("p j c -> p c j")))
            ch = choice[:, :, :].rearrange("p c j -> p (c j)")
            nc.vector.tensor_tensor(oh[:, :, :], iota_e[:, :].unsqueeze(2).broadcast_to([P, E, A]),
                                    ch.unsqueeze(1).broadcast_to([P, E, A]),
                                    ALU.is_equal).then_inc(oh_ok, 1)
            picked = val[:, :, :].rearrange("p c j -> p (c j)")
            link(nc.vector.tensor_copy(gate_hi[:, :], picked))
            link(nc.vector.tensor_tensor(gate_lo[:, :], picked, gate_hi[:, :].bitcast(F32), ALU.subtract))
            dve.wait_ge(rank_ps, 1)
            EA = E * A
            within, total = ps_rank[:, 0:EA], ps_rank[:, EA:2 * EA]

            def flat(t):
                return t[:, :, :].rearrange("p e a -> p (e a)")

            link(nc.vector.tensor_tensor_scan(flat(run), flat(carry), total, 0.0, ALU.mult, ALU.add))
            nc.vector.tensor_scalar(more[:, :].unsqueeze(2), run[0:1, :, A - 1:A], -float((TPE - 1) * P),
                                    0.0, ALU.add, ALU.max).then_inc(more_ok, 1)
            dve.wait_ge(more_ok, 1)
            link(nc.vector.tensor_tensor(flat(run), flat(run), total, ALU.subtract))
            link(nc.vector.tensor_tensor(flat(rk), flat(run), within, ALU.add))
            link(nc.vector.tensor_tensor(flat(rk), flat(rk), flat(oh), ALU.mult))
            link(nc.vector.reduce_sum(r1[:, :], rk[:, :, :].rearrange("p e a -> p a e"), AX))
            nc.vector.tensor_scalar(over[:, :], r1[:, :], float(CAP), float(FAR), ALU.is_gt, ALU.mult)
            link(nc.vector.scalar_tensor_tensor(slot_f[:, :], ch, float(CAP), r1[:, :], ALU.mult, ALU.add))
            link(nc.vector.scalar_tensor_tensor(slot[:, :], over[:, :], -1.0, slot_f[:, :], ALU.add, ALU.add))
            nc.vector.tensor_scalar(slot_i[:, 0, :], slot[:, :], 7, None, ALU.arith_shift_right)
            link(nc.vector.tensor_scalar(slot_i[:, 1, :], slot[:, :], P - 1, None, ALU.bitwise_and))
            nc.vector.tensor_copy(slot_tp[:, :, :], slot_i[:, :, :]).then_inc(slot_ok, 1)
            dve.wait_ge(slot_ok, 1)
            toks = token1[:, :, :].rearrange("p c j -> p (c j)")
            AQ = A // 4
            for q in range(4):
                a = slice(q * AQ, (q + 1) * AQ)
                wide = [P, AQ, NT]
                link(nc.vector.tensor_tensor(
                    pick_t[:, a, :], iota_t[:, :].unsqueeze(1).broadcast_to(wide),
                    slot_tp[:, 0, a].unsqueeze(2).broadcast_to(wide), ALU.is_equal))
                last = nc.vector.tensor_tensor(what_tok[:, a, :], pick_t[:, a, :],
                                               toks[:, a].unsqueeze(2).broadcast_to(wide), ALU.mult)
                b = slice(q * AQ, min((q + 1) * AQ, A - POOL_PICKS))
                if b.start < b.stop:
                    last = nc.vector.tensor_tensor(
                        pick_p[:, b, :], iota_p[:, :].unsqueeze(1).broadcast_to([P, b.stop - b.start, P]),
                        slot_tp[:, 1, b].unsqueeze(2).broadcast_to([P, b.stop - b.start, P]), ALU.is_equal)
                last.then_inc(pick_ok, 1)

            def gate_picks(q):
                a = slice(q * AQ, (q + 1) * AQ)
                for v, t in enumerate((gate_hi, gate_lo)):
                    last = nc.vector.tensor_tensor(
                        what_gate[:, a, v, :], pick_t[:, a, :],
                        t[:, a].bitcast(F32).unsqueeze(2).broadcast_to([P, AQ, NT]), ALU.mult)
                last.then_inc(gate_pick_ok, 1)

            for q in range(4):
                gate_picks(q)
            dve.wait_ge(slot_ps, 1)
            link(nc.vector.tensor_copy(got[:, 0, :], ps_slot[:, 0:NT]))
            nc.vector.tensor_scalar(src_row[:, :], got[:, 0, :], -1.0, 0.0, ALU.add,
                                    ALU.max).then_inc(lists_ok, 1)
            link(nc.vector.scalar_tensor_tensor(empty[:, :], got[:, 0, :], 0.0, spare[:, :],
                                                ALU.is_equal, ALU.mult))
            nc.vector.scalar_tensor_tensor(dst_row[:, :], got[:, 0, :], -1.0, empty[:, :], ALU.add,
                                           ALU.add).then_inc(lists_ok, 1)

            def w0_low(u):
                a, b = UNIT[u]
                dve.wait_ge(whi_ok, u + 1)
                nc.vector.tensor_tensor(wlo[:, 0, a:b], raw[:, a:b], whi[:, 0, a:b].bitcast(F32),
                                        ALU.subtract).then_inc(wlo0_ok, 1)

            for u in range(KH):
                w0_low(u)

            def x_low(i, s, n):
                dve.wait_ge(xhi_ok, tile(i, s) + 1)
                nc.vector.tensor_tensor(xlo[:, x_buffer(s), :], ps_xT[:, :],
                                        xhi[:, x_buffer(s), :].bitcast(F32), ALU.subtract).then_inc(xlo_ok, n)

            def next_w_low(i, s):
                if 1 <= known(i, s) <= NT - TPE:
                    a, b = UNIT[(s - 1) % NU]
                    half = ((s - 1) // NU + 1) % 2
                    dve.wait_ge(whi_ok, tile(i, s) + NU)
                    nc.vector.tensor_tensor(wlo[:, half, a:b], raw[:, a:b], whi[:, half, a:b].bitcast(F32),
                                            ALU.subtract).then_inc(wlo_ok, 1)

            def step(i, s, n):
                if known(i, s) + n < NT:
                    x_low(i, s + n, n)
                dve.wait_ge(silu_ok, tile(i, s) + 1)
                nc.vector.tensor_tensor(h_sb[:, 0:I], g_sb[:, :], ps_up[:, 0:I], ALU.mult).then_inc(h_ok, n)
                for t in range(s, s + n):
                    next_w_low(i, t)
                dve.wait_ge(hhi_ok, tile(i, s) + 1)
                nc.vector.tensor_tensor(hlo[:, :], ps_hT[:, 0:IP], hhi[:, :].bitcast(F32),
                                        ALU.subtract).then_inc(hlo_ok, n)

            x_low(0, 0, 1)
            dve.wait_ge(slot_gates_ps, 4)
            link(nc.vector.tensor_copy(got[:, 1:3, :], ps_slot_gate[:, 0:2 * NT]
                                       .rearrange("p (v t) -> p v t", v=2)))
            nc.vector.tensor_tensor(w_slot[:, :], got[:, 1, :], got[:, 2, :], ALU.add).then_inc(w_slot_ok, 1)
            w0_low(KH)
            over_slots(dve, step)

        @block.tensor
        def _(pe):
            def router(g):
                pe.wait_ge(xT_in[g], 16)
                for k in range(KH):
                    last = nc.tensor.matmul(ps_xrT[g][k * Q:(k + 1) * Q, :], wr_sb[:, k, :],
                                            xT_sb[:, g, k, :], start=True, stop=True)
                last.then_inc(xrT_ps, 1)

            def turn(g):
                pe.wait_ge(xrT_ok, g + 1)
                if g >= 2:
                    pe.wait_ge(xr_ok, g - 1)
                for j in range(GR):
                    last = nc.tensor.transpose(ps_xr[g % 2][:, j * P:(j + 1) * P],
                                               xrT[:, g, j * P:(j + 1) * P], ident[:, :])
                last.then_inc(xr_ps, 1)

            def logits(g):
                pe.wait_ge(xr_ok, g + 1)
                if g < NG - 1:
                    pe.wait_ge(wbd_ok, 2 * (g + 1))
                else:
                    pe.wait_ge(wbd_last_ok, 2)
                for j in range(g * GR, (g + 1) * GR):
                    c = j % HALF * E
                    last = nc.tensor.matmul(ps_lg[j // HALF][:, c:c + E], wbd[:, j, :], xr[:, j, :],
                                            start=True, stop=True)
                last.then_inc(lg_ps, 1)

            def condition(j):
                pe.wait_ge(x_in[j % XR], 16 * (j // XR + 1))
                if j >= XR:
                    pe.wait_ge(xf_ok, j - XR + 1)
                nc.tensor.matmul(ps_xf[j % XR][:, :], wbd[:, j, :], x_sb[:, j, :],
                                 start=True, stop=True).then_inc(xf_ps, 1)

            pe.wait_ge(wr_in, 16)
            pe.wait_ge(consts, 4)
            for g in range(NG + 1):
                if g < NG:
                    router(g)
                if g >= 1:
                    turn(g - 1)
            BEFORE_RANKS, BEFORE_SLOTS = 3, TT
            for g in range(NG):
                if g == NG - 1:
                    condition(0)
                logits(g)
            for j in range(1, BEFORE_RANKS):
                condition(j)
            pe.wait_ge(consts, CONSTS)
            pe.wait_ge(oh_ok, 1)
            o = oh[:, :, :].rearrange("p e a -> p (e a)")
            nc.tensor.matmul(ps_rank[:, 0:E * A], upper[:, :], o, start=True, stop=True)
            nc.tensor.matmul(ps_rank[:, E * A:2 * E * A], ones[:, :], o,
                             start=True, stop=True).then_inc(rank_ps, 1)
            for j in range(BEFORE_RANKS, BEFORE_SLOTS):
                condition(j)
            for a in range(A):
                if a % (A // 4) == 0:
                    pe.wait_ge(pick_ok, a // (A // 4) + 1)
                if a >= A - POOL_PICKS:
                    pe.wait_ge(pool_pick_ok, a - (A - POOL_PICKS) + 1)
                last = nc.tensor.matmul(ps_slot[:, 0:NT], pick_p[:, a, :], what_tok[:, a, :],
                                        start=(a == 0), stop=(a == A - 1))
            last.then_inc(slot_ps, 1)
            def slot_gates(q):
                pe.wait_ge(gate_pick_ok, q + 1)
                for a in range(q * (A // 4), (q + 1) * (A // 4)):
                    last = nc.tensor.matmul(ps_slot_gate[:, 0:2 * NT], pick_p[:, a, :],
                                            what_gate[:, a, :, :].rearrange("p v t -> p (v t)"),
                                            start=(a == 0), stop=(a == A - 1))
                last.then_inc(slot_gates_ps, 1)

            for q in range(2):
                slot_gates(q)
            for j in range(BEFORE_SLOTS, TT):
                condition(j)

            pe.wait_ge(xf_ok, TT)

            def x_turn(i, s, n):
                pe.wait_ge(xg_in[s % TPE], (expert(i, s) + 1) * 16)
                if known(i, s) > 0:
                    pe.wait_ge(xlo_ok, tile(i, s) - n + 1)
                for k in range(KH):
                    last = nc.tensor.transpose(ps_xT[:, k * P:(k + 1) * P],
                                               xg[:, s % TPE, k * P:(k + 1) * P], ident[:, :])
                last.then_inc(xT_ps, n)

            def gate_up(s, n, ks):
                half, b = half_of(s), x_buffer(s)
                for k in ks:
                    g, u = k * 2 * I, k * 2 * I + I
                    c = slice(k * P, (k + 1) * P)
                    for q, (left, right) in enumerate(((xhi, whi), (xhi, wlo), (xlo, whi))):
                        for ps, o in ((ps_gate, g), (ps_up, u)):
                            last = nc.tensor.matmul(ps[:, 0:I], left[:, b, c], right[:, half, o:o + I],
                                                    start=(k == 0 and q == 0), stop=(k == KH - 1 and q == 2))
                if KH - 1 in ks:
                    last.then_inc(gu_ps, n)

            def down(i, s, n):
                half = half_of(s)
                pe.wait_ge(hlo_ok, tile(i, s) + 1)
                if known(i, s) == 0:
                    pe.wait_ge(wlo0_ok, NU)
                elif s % TPE == 0:
                    pe.wait_ge(wlo_ok, tile(i, s))
                if known(i, s) > 0:
                    pe.wait_ge(y_ok, tile(i, s))
                for c in range(KI):
                    o = DOWN + c * H
                    for q, (left, right) in enumerate(((hhi, whi), (hhi, wlo), (hlo, whi))):
                        last = nc.tensor.matmul(ps_y[:, :], left[:, c * P:(c + 1) * P],
                                                right[:, half, o:o + H],
                                                start=(c == 0 and q == 0), stop=(c == KI - 1 and q == 2))
                last.then_inc(y_ps, n)

            def step(i, s, n):
                pe.wait_ge(xlo_ok, tile(i, s) + 1)
                if known(i, s) == 0:
                    pe.wait_ge(wlo0_ok, KH)
                elif s % TPE == 0:
                    pe.wait_ge(wlo_ok, tile(i, s) - 3)
                gate_up(s, n, (0, 1))
                if known(i, s) + n < NT:
                    x_turn(i, s + n, n)
                if s % TPE == 0 and known(i, s) > 0:
                    pe.wait_ge(wlo_ok, tile(i, s) - 1)
                gate_up(s, n, (2, 3))
                if known(i, s) > 0:
                    tile_before(pe, i, s, down)
                pe.wait_ge(h_ok, tile(i, s) + 1)
                for c in range(KI):
                    last = nc.tensor.transpose(ps_hT[:, c * P:(c + 1) * P], h_sb[:, c * P:(c + 1) * P],
                                               ident[:, :])
                last.then_inc(hT_ps, n)

            pe.wait_ge(more_ok, 1)
            x_turn(0, 0, 1)
            for q in range(2, 4):
                slot_gates(q)
            over_slots(pe, step)
            tile_before(pe, PASSES, NT - PASS * PASSES, down)


def kernel(x, itok_B_1_198, L0_cond_weights, L0_ffn_Wr, L0_ffn_Wg, L0_ffn_Wu, L0_ffn_Wd):
    import numpy as np
    import concourse.bacc as bacc
    from concourse.bass_utils import run_bass_kernel_spmd

    arrays = {
        "x": np.asarray(x).reshape(B * C, H),
        "xT": np.asarray(x).reshape(B * C, H).T,
        "cond": np.asarray(itok_B_1_198).reshape(TT, 2).T,
        "wcond": np.asarray(L0_cond_weights).reshape(S * C, D),
        "wr": np.asarray(L0_ffn_Wr).T,
        "wg": np.asarray(L0_ffn_Wg).transpose(0, 2, 1),
        "wu": np.asarray(L0_ffn_Wu).transpose(0, 2, 1),
        "wd": np.asarray(L0_ffn_Wd).transpose(0, 2, 1),
    }
    arrays = {name: np.ascontiguousarray(a) for name, a in arrays.items()}
    nc = bacc.Bacc("TRN2", target_bir_lowering=False, num_devices=1)
    ins = [nc.dram_tensor(name, a.shape, mybir.dt.from_np(a.dtype), kind="ExternalInput").ap()
           for name, a in arrays.items()]
    out = nc.dram_tensor("out", (N + CAP, H), F32, kind="ExternalOutput").ap()
    build(nc, *ins, out)
    r = run_bass_kernel_spmd(nc, [arrays], core_ids=[0])
    return r.results[0]["out"][0:N].reshape(B, C, H)
```

```python
from contextlib import ExitStack

import concourse.bass as bass
from concourse import mybir

B, C, D, H = 32, 64, 64, 512
N = B * D
S = 200
E, I = 8, 352
TOP = 2
CAP = int(1.25 * (N * TOP / E))
P = 128
Q = 32
TT = N // P
KH = H // P
KI = (I + P - 1) // P
IP = KI * P
IR = I - (KI - 1) * P
TPE = CAP // P
NT = E * TPE
A = TOP * TT
FAR = 100000

UNIT = [(k * 2 * I, (k + 1) * 2 * I) for k in range(KH)] + [(KH * 2 * I, KH * 2 * I + KI * H)]
NU = len(UNIT)
DOWN = UNIT[-1][0]
WC = UNIT[-1][1]

XR = 4
GR = 4
NG = TT // GR
HALF = TT // 2
HG = H + E
POOL_PICKS = 12
BEFORE_RANKS = 6
KEEP_WARM = 5

PASS = 2 * TPE
FIRST = TPE + 1
PASSES = (NT - FIRST) // PASS
AHEAD = TPE

F32 = mybir.dt.float32
F32R = mybir.dt.float32r
BF16 = mybir.dt.bfloat16
I32 = mybir.dt.int32
U32 = mybir.dt.uint32
U16 = mybir.dt.uint16
ALU = mybir.AluOpType
ACT = mybir.ActivationFunctionType
AX = mybir.AxisListType.X


def build(nc, x, cond, wcond, wr, wgu, wd, out):
    xf_dram = nc.dram_tensor("xf_dram", (N, HG), F32, kind="Internal").ap()
    ctx = ExitStack()
    with ctx:
        def sb(name, shape, dt=F32):
            return ctx.enter_context(nc.sbuf_tensor(name, shape, dt))

        def pb(name):
            return ctx.enter_context(nc.psum_tensor(name, [P, 512], F32))

        def sem(name):
            return ctx.enter_context(nc.semaphore(name))

        ident = sb("ident", [P, P])
        upper = sb("upper", [P, P], BF16)
        ones = sb("ones", [P, P], BF16)
        iota_e = sb("iota_e", [P, E])
        iota_p = sb("iota_p", [P, P])
        iota_t = sb("iota_t", [P, NT])
        row_in_c = sb("row_in_c", [P, 1])
        token1 = sb("token1", [P, TOP, TT])
        spare = sb("spare", [P, NT])
        carry = sb("carry", [P, E, A])

        condb = sb("condb", [P, TT], I32)
        cidx = sb("cidx", [P, TT], U32)
        wc_sb = sb("wc_sb", [P, TT, D])
        wbd = sb("wbd", [P, TT, 2 * D])
        wr_sb = sb("wr_sb", [P, KH, Q])
        x_sb = sb("x_sb", [P, TT, H])
        xrT = sb("xrT", [P, NG, GR * P])
        xr = sb("xr", [P, TT, E])
        lg = sb("lg", [P, TT, E])
        mx = sb("mx", [P, TT])
        ex = sb("ex", [P, TT, E])
        sm = sb("sm", [P, TT])
        gate = sb("gate", [P, TT, E])
        v8 = sb("v8", [P, TT, 8])
        i8 = sb("i8", [P, TT, 8], U32)
        choice = sb("choice", [P, TOP, TT])
        oh = sb("oh", [P, E, A], BF16)
        run = sb("run", [P, E, A])
        more = sb("more", [1, E], U16)
        rk = sb("rk", [P, E, A])
        r1 = sb("r1", [P, A])
        over = sb("over", [P, A])
        slot_f = sb("slot_f", [P, A])
        slot = sb("slot", [P, A], I32)
        slot_i = sb("slot_i", [P, 2, A], I32)
        slot_tp = sb("slot_tp", [P, 2, A])
        pick_t = sb("pick_t", [P, A, NT])
        got = sb("got", [P, NT])
        empty = sb("empty", [P, NT])
        src_row = sb("src_row", [P, NT], U32)
        dst_row = sb("dst_row", [P, NT], U32)

        raw = sb("raw", [P, WC])
        whi = sb("whi", [P, 2, WC], F32R)
        wlo = sb("wlo", [P, 2, WC], F32R)
        xhi = sb("xhi", [P, 3, H], F32R)
        xlo = sb("xlo", [P, 3, H], F32R)
        g_sb = sb("g_sb", [P, I])
        h_sb = sb("h_sb", [P, IP])
        hhi = sb("hhi", [P, IP], F32R)
        hlo = sb("hlo", [P, IP], F32R)

        tiles = sb("tiles", [P, TT * HG])
        tT_sb = tiles[:, 0:TT * H].rearrange("p (g k c) -> p g k c", g=NG, k=KH)
        xf_sb = tiles[:, :].rearrange("p (j h) -> p j h", h=HG)
        xg = tiles[:, 0:TPE * HG].rearrange("p (t h) -> p t h", h=HG)
        y_sb = tiles[:, TPE * HG:TPE * (HG + H)].rearrange("p (t h) -> p t h", h=H)
        pick_p = whi[:, 1, 0:A * P].rearrange("p (a q) -> p a q", q=P)
        what = wlo[:, 1, 0:A * NT].rearrange("p (a t) -> p a t", t=NT)

        bank = [pb(f"bank{n}") for n in range(8)]
        ps_tT = ps_xf = bank[0:XR]
        ps_xrT, ps_xr, ps_lg = bank[5], bank[6], (bank[4], bank[7])
        ps_rank, ps_slot = bank[5], bank[6]
        ps_gate, ps_up, ps_hT, ps_xT, ps_y = bank[5], bank[6], bank[7], bank[2], bank[0]

        consts = sem("consts")
        CONSTS = 15
        pad_ok = sem("pad_ok")
        wr_clear = sem("wr_clear")
        wbd_clear = sem("wbd_clear")
        cond_in = sem("cond_in")
        wr_in = sem("wr_in")
        x_in = [sem(f"x_in{m}") for m in range(TT // 2)]
        cidx_ok = sem("cidx_ok")
        wc_in = [sem(f"wc_in{g}") for g in range(NG)]
        wbd_ok = sem("wbd_ok")
        wbd_last_ok = sem("wbd_last_ok")
        tT_ps = sem("tT_ps")
        tT_even_ok = sem("tT_even_ok")
        tT_odd_ok = sem("tT_odd_ok")
        xrT_ps = sem("xrT_ps")
        xrT_ok = sem("xrT_ok")
        xr_ps = sem("xr_ps")
        xr_ok = sem("xr_ok")
        lg_ps = sem("lg_ps")
        sub_ok = sem("sub_ok")
        ex_ok = sem("ex_ok")
        route = sem("route")
        gate_cols_ok = sem("gate_cols_ok")
        xf_ps = sem("xf_ps")
        xf_ok = sem("xf_ok")
        xf_out = sem("xf_out")
        oh_ok = sem("oh_ok")
        rank_ps = sem("rank_ps")
        more_ok = sem("more_ok")
        slot_ok = sem("slot_ok")
        pick_ok = sem("pick_ok")
        pool_pick_ok = sem("pool_pick_ok")
        slot_ps = sem("slot_ps")
        lists_ok = sem("lists_ok")
        out_init = sem("out_init")
        raw_in = [sem(f"raw_in{u}") for u in range(NU)]
        whi_ok = sem("whi_ok")
        wlo0_ok = sem("wlo0_ok")
        wlo_ok = sem("wlo_ok")
        xg_in = [sem(f"xg_in{t}") for t in range(TPE)]
        xT_ps = sem("xT_ps")
        xhi_ok = sem("xhi_ok")
        xlo_ok = sem("xlo_ok")
        gu_ps = sem("gu_ps")
        silu_warm = sem("silu_warm")
        silu_ok = sem("silu_ok")
        h_ok = sem("h_ok")
        hT_ps = sem("hT_ps")
        hhi_ok = sem("hhi_ok")
        hlo_ok = sem("hlo_ok")
        y_ps = sem("y_ps")
        y_ok = sem("y_ok")
        y_out = [sem(f"y_out{t}") for t in range(TPE)]

        block = ctx.enter_context(nc.Block())

        x_t = x.rearrange("(j p) h -> p j h", p=P)
        xf_t = xf_dram.rearrange("(j p) h -> p j h", p=P)
        out_t = out[0:N, :].rearrange("(j p) h -> p j h", p=P)

        def tile(i, s):
            return i * PASS + s

        def known(i, s):
            return tile(i, s) if isinstance(i, int) else FIRST

        def expert(i, s):
            return i * (PASS // TPE) + s // TPE

        def half_of(s):
            return (s // TPE) % 2

        def x_buffer(s):
            return 2 if s % TPE == TPE - 1 else s % TPE % 2

        def passed_over(eng, i, s, full, short):
            more_there = eng.value_load(more[0:1, bass.ds(expert(i, s), 1)])
            with eng.If(more_there > 0):
                full()
            with eng.Else():
                short()

        def over_slots(eng, step):
            def steps(i, s):
                if s % TPE < TPE - 2:
                    step(i, s, 1)
                elif s % TPE == TPE - 2:
                    def both():
                        step(i, s, 1)
                        step(i, s + 1, 1)

                    passed_over(eng, i, s, both, lambda: step(i, s, 2))

            for s in range(FIRST):
                steps(0, s)
            with eng.Fori(0, PASSES) as i:
                for s in range(FIRST, FIRST + PASS):
                    steps(i, s)
            for s in range(FIRST, NT - PASS * PASSES):
                steps(PASSES, s)

        def tile_before(eng, i, s, do):
            if s % TPE == 0:
                passed_over(eng, i, s - 1, lambda: do(i, s - 1, 1), lambda: do(i, s - 2, 2))
            else:
                do(i, s - 1, 1)

        @block.sync
        def _(sp):
            for half in range(2):
                sp.dma_start(condb[half * C:(half + 1) * C, :],
                             cond[half:half + 1, :].broadcast_to([C, TT])).then_inc(cond_in, 16)

            def load_x(m):
                js = slice(m * 2, m * 2 + 2)
                sp.dma_start(x_sb[:, js, :], x_t[:, js, :]).then_inc(x_in[m], 16)

            load_x(0)
            sp.wait_ge(wr_clear, 1)
            sp.dma_start(wr_sb[:, :, 0:E],
                         wr.rearrange("(k p) e -> p k e", p=P)).then_inc(wr_in, 16)
            for m in range(1, TT // 2):
                if m >= 2:
                    sp.wait_ge(x_in[m - 2], 16)
                load_x(m)

            def load_unit(e, u):
                a, b = UNIT[u]
                if u < KH:
                    sp.dma_start(raw[:, a:b], wgu[bass.ds(e, 1), u * P:(u + 1) * P, :]
                                 .rearrange("o p i -> (o p) i")).then_inc(raw_in[u], 16)
                else:
                    full = (KI - 1) * P
                    sp.dma_start(raw[:, a:a + (KI - 1) * H].rearrange("p (c h) -> p c h", c=KI - 1),
                                 wd[bass.ds(e, 1), 0:full, :]
                                 .rearrange("o (c p) h -> p (o c) h", p=P)).then_inc(raw_in[u], 16)
                    sp.dma_start(raw[0:IR, a + (KI - 1) * H:b], wd[bass.ds(e, 1), full:I, :]
                                 .rearrange("o p h -> (o p) h")).then_inc(raw_in[u], 16)

            sp.wait_ge(wc_in[NG - 1], 16 * GR)
            sp.wait_ge(pad_ok, 1)
            for u in range(NU):
                load_unit(0, u)
            sp.wait_ge(gate_cols_ok, 1)
            with sp.Fori(0, TT // 2 - 1) as m:
                sp.wait_ge(xf_ok, m * 2 + 2)
                sp.dma_start(xf_t[:, bass.ds(m * 2, 2), :],
                             xf_sb[:, bass.ds(m * 2, 2), :]).then_inc(xf_out, 16)
            for j in range(TT - 2, TT):
                sp.wait_ge(xf_ok, j + 1)
                sp.dma_start(xf_t[:, j:j + 1, :], xf_sb[:, j:j + 1, :]).then_inc(xf_out, 16)
            sp.wait_ge(xg_in[0], 16)
            for u in range(NU):
                sp.wait_ge(wlo0_ok, u + 1)
                load_unit(1, u)
            for t in range(AHEAD):
                sp.wait_ge(xg_in[t], 16)
            for m in range(TT // 2):
                sp.wait_ge(x_in[m], 16)
            for q in range(TT // XR):
                sp.dma_start(out_t[:, q * XR:(q + 1) * XR, :],
                             x_sb[:, q * XR:(q + 1) * XR, :]).then_inc(out_init, 16)
            sp.dma_start(out[N:N + CAP, :].rearrange("(t p) h -> p t h", p=P),
                         x_sb[:, 0:TPE, :]).then_inc(out_init, 16)
            with sp.Fori(2, E) as e:
                for u in range(NU):
                    sp.wait_ge(wlo_ok, (e - 2) * NU + u + 1)
                    load_unit(e, u)

        @block.gpsimd
        def _(pool):
            for half in range(2):
                nc.gpsimd.iota(row_in_c[half * C:(half + 1) * C, :], [[0, 1]], base=0,
                               channel_multiplier=1,
                               allow_small_or_imprecise_dtypes=True).then_inc(consts, 1)
                pool.wait_ge(consts, half + 1)
            nc.gpsimd.memset(raw[IR:P, DOWN + (KI - 1) * H:WC], 0.0).then_inc(pad_ok, 1)
            pool.wait_ge(pad_ok, 1)
            nc.gpsimd.memset(ident[:, :], 0.0).then_inc(consts, 1)
            pool.wait_ge(consts, 3)
            nc.gpsimd.affine_select(out=ident[:, :], in_=ident[:, :], compare_op=ALU.not_equal,
                                    fill=1.0, base=0, pattern=[[-1, P]],
                                    channel_multiplier=1).then_inc(consts, 1)
            pool.wait_ge(cidx_ok, 1)
            for j in range(TT):
                nc.gpsimd.indirect_dma_start(
                    out=wc_sb[:, j, :], out_offset=None, in_=wcond[:, :],
                    in_offset=bass.IndirectOffsetOnAxis(ap=cidx[:, j:j + 1], axis=0),
                ).then_inc(wc_in[j // GR], 16)

            nc.gpsimd.memset(upper[:, :], 1.0).then_inc(consts, 1)
            nc.gpsimd.memset(carry[:, :, :], 1.0).then_inc(consts, 1)
            pool.wait_ge(consts, 6)
            nc.gpsimd.affine_select(out=upper[:, :], in_=upper[:, :], compare_op=ALU.is_ge,
                                    fill=0.0, base=0, pattern=[[1, P]],
                                    channel_multiplier=-1).then_inc(consts, 1)
            nc.gpsimd.memset(carry[:, :, 0:1], 0.0).then_inc(consts, 1)
            nc.gpsimd.memset(ones[:, :], 1.0).then_inc(consts, 1)
            nc.gpsimd.memset(h_sb[:, I:IP], 0.0).then_inc(consts, 1)
            for t, pattern, base, step in (
                    (iota_e[:, :], [[1, E]], 0, 0), (iota_p[:, :], [[1, P]], 0, 0),
                    (iota_t[:, :], [[1, NT]], 0, 0), (token1[:, :, :], [[0, TOP], [P, TT]], 1, 1),
                    (spare[:, :], [[0, E], [P, TPE]], N + 1, 1)):
                nc.gpsimd.iota(t, pattern, base=base, channel_multiplier=step,
                               allow_small_or_imprecise_dtypes=True).then_inc(consts, 1)

            pool.wait_ge(slot_ok, 1)
            for a in range(A - POOL_PICKS, A):
                nc.gpsimd.tensor_scalar(pick_p[:, a, :], iota_p[:, :], slot_tp[:, 1, a:a + 1], None,
                                        ALU.is_equal).then_inc(pool_pick_ok, 1)

            pool.wait_ge(lists_ok, 1)
            pool.wait_ge(xf_out, 16 * (TT // 2 + 1))

            def gather(n):
                if n >= TPE:
                    pool.wait_ge(y_ok, n - TPE + 1)
                nc.gpsimd.indirect_dma_start(
                    out=xg[:, n % TPE, :], out_offset=None, in_=xf_dram[:, :],
                    in_offset=bass.IndirectOffsetOnAxis(ap=src_row[:, n:n + 1], axis=0),
                ).then_inc(xg_in[n % TPE], 16)

            def scatter(n):
                if n % TPE == 0 and n > 0:
                    for q in range(TPE):
                        pool.wait_ge(y_out[q], 16 * (n // TPE))
                pool.wait_ge(y_ok, n + 1)
                nc.gpsimd.indirect_dma_start(
                    out=out[:, :], in_=y_sb[:, n % TPE, :], in_offset=None,
                    out_offset=bass.IndirectOffsetOnAxis(ap=dst_row[:, n:n + 1], axis=0),
                    compute_op=ALU.add,
                ).then_inc(y_out[n % TPE], 16)

            for n in range(AHEAD):
                gather(n)
            pool.wait_ge(out_init, 16 * (TT // XR + 1))
            pool.wait_ge(lists_ok, 2)
            for n in range(NT):
                if n + AHEAD < NT:
                    gather(n + AHEAD)
                scatter(n)
            for t in range(TPE):
                pool.wait_ge(y_out[t], 16 * E)

        @block.scalar
        def _(act):
            def exps(h):
                act.wait_ge(sub_ok, h + 1)
                js = slice(h * HALF, (h + 1) * HALF)
                nc.scalar.activation(ex[:, js, :], lg[:, js, :], ACT.Exp).then_inc(ex_ok, 1)

            def xf_copy(n, s):
                act.wait_ge(xf_ps, n + 1)
                nc.scalar.activation(xf_sb[:, bass.ds(n, 1), 0:H], ps_xf[s][:, :].unsqueeze(1),
                                     ACT.Copy).then_inc(xf_ok, 1)

            for j in range(0, TT, 2):
                act.wait_ge(tT_ps, j + 1)
                nc.scalar.activation(tT_sb[:, j // GR, :, j % GR * P:(j % GR + 1) * P],
                                     ps_tT[j % XR][:, :].rearrange("p (k c) -> p k c", k=KH),
                                     ACT.Copy).then_inc(tT_even_ok, 1)
            exps(0)
            js = slice((NG - 1) * GR, TT)
            act.wait_ge(wbd_clear, 1)
            act.wait_ge(wc_in[NG - 1], 16 * GR)
            for half in range(2):
                rows = slice(half * C, (half + 1) * C)
                nc.scalar.activation(wbd[rows, js, half * D:(half + 1) * D], wc_sb[rows, js, :],
                                     ACT.Copy).then_inc(wbd_last_ok, 1)
            xf_copy(0, 0)
            exps(1)
            for n in range(1, XR):
                xf_copy(n, n)
            with act.Fori(1, TT // XR) as i:
                for s in range(XR):
                    xf_copy(i * XR + s, s)

            def w_high(u, half, e):
                a, b = UNIT[u]
                act.wait_ge(raw_in[u], (e + 1) * (16 if u < KH else 32))
                nc.scalar.activation(whi[:, half, a:b], raw[:, a:b], ACT.Copy).then_inc(whi_ok, 1)

            for u in range(NU):
                w_high(u, 0, 0)

            def x_high(i, s, n):
                act.wait_ge(xT_ps, tile(i, s) + 1)
                nc.scalar.activation(xhi[:, x_buffer(s), :], ps_xT[:, :],
                                     ACT.Copy).then_inc(xhi_ok, n)

            def next_w_high(i, s):
                if 1 <= known(i, s) <= NT - TPE:
                    w_high((s - 1) % NU, ((s - 1) // NU + 1) % 2, expert(i, s - 1) + 1)

            def y_scale(i, s, n):
                act.wait_ge(y_ps, tile(i, s) + 1)
                if known(i, s) >= TPE:
                    act.wait_ge(y_out[s % TPE], expert(i, s) * 16)
                gates = xg[:, s % TPE, bass.ds(H + expert(i, s), 1)]
                nc.scalar.activation(y_sb[:, s % TPE, :], ps_y[:, :], ACT.Copy,
                                     scale=gates).then_inc(y_ok, n)

            def step(i, s, n):
                if known(i, s) + n < NT:
                    x_high(i, s + n, n)
                act.wait_ge(gu_ps, tile(i, s) + 1)
                nc.scalar.activation(g_sb[:, :], ps_gate[:, 0:I], ACT.Silu).then_inc(silu_ok, n)
                for t in range(s, s + n):
                    next_w_high(i, t)
                if known(i, s) > 0:
                    tile_before(act, i, s, y_scale)
                act.wait_ge(hT_ps, tile(i, s) + 1)
                nc.scalar.activation(hhi[:, :], ps_hT[:, 0:IP], ACT.Copy).then_inc(hhi_ok, n)

            act.wait_ge(consts, 4)
            nc.scalar.activation(g_sb[:, 0:1], ident[:, 0:1], ACT.Silu).then_inc(silu_warm, 1)
            x_high(0, 0, 1)
            act.wait_ge(silu_warm, 1)
            act.wait_ge(more_ok, 1)
            over_slots(act, step)
            tile_before(act, PASSES, NT - PASS * PASSES, y_scale)

        @block.vector
        def _(dve):
            nc.vector.memset(wr_sb[:, :, :], 0.0).then_inc(wr_clear, 1)
            dve.wait_ge(cond_in, 32)
            dve.wait_ge(consts, 2)
            nc.vector.tensor_scalar(cidx[:, :], condb[:, :], float(C), row_in_c[:, :], ALU.mult,
                                    ALU.add).then_inc(cidx_ok, 1)

            nc.vector.memset(wbd[:, :, :], 0.0).then_inc(wbd_clear, 1)
            dve.wait_ge(wbd_clear, 1)

            def diagonal(g):
                js = slice(g * GR, (g + 1) * GR)
                dve.wait_ge(wc_in[g], 16 * GR)
                for half in range(2):
                    rows = slice(half * C, (half + 1) * C)
                    nc.vector.tensor_copy(wbd[rows, js, half * D:(half + 1) * D],
                                          wc_sb[rows, js, :]).then_inc(wbd_ok, 1)

            chain = [0]

            def link(ins):
                chain[0] += 1
                ins.then_inc(route, 1)
                dve.wait_ge(route, chain[0])

            def gates(h):
                js = slice(h * HALF, (h + 1) * HALF)
                wide = [P, HALF, E]
                dve.wait_ge(lg_ps, (h + 1) * (NG // 2))
                lg_v = ps_lg[h][:, 0:HALF * E].rearrange("p (j e) -> p j e", e=E)
                link(nc.vector.reduce_max(mx[:, js], lg_v, AX))
                nc.vector.tensor_tensor(lg[:, js, :], lg_v,
                                        mx[:, js].unsqueeze(2).broadcast_to(wide),
                                        ALU.subtract).then_inc(sub_ok, 1)
                dve.wait_ge(ex_ok, h + 1)
                link(nc.vector.reduce_sum(sm[:, js], ex[:, js, :], AX))
                link(nc.vector.reciprocal(sm[:, js], sm[:, js]))
                link(nc.vector.tensor_tensor(gate[:, js, :], ex[:, js, :],
                                             sm[:, js].unsqueeze(2).broadcast_to(wide), ALU.mult))
                for j in range(h * HALF, (h + 1) * HALF):
                    last = nc.vector.max(v8[:, j, :], gate[:, j, :])
                link(last)
                for j in range(h * HALF, (h + 1) * HALF):
                    last = nc.vector.max_index(i8[:, j, :], v8[:, j, :], gate[:, j, :])
                link(last)

            def xrT_copy(g):
                dve.wait_ge(xrT_ps, g + 1)
                nc.vector.tensor_copy(xrT[:, g, :], ps_xrT[:, :]).then_inc(xrT_ok, 1)

            def xr_sum(g):
                dve.wait_ge(xr_ps, g + 1)
                js = slice(g * GR, (g + 1) * GR)
                parts = ps_xr[:, :].rearrange("p (j k c) -> p j c k", j=GR, k=KH)
                nc.vector.reduce_sum(xr[:, js, :], parts[:, :, 0:E, :], AX).then_inc(xr_ok, 1)

            def tT_copy(j):
                dve.wait_ge(tT_ps, j + 1)
                nc.vector.tensor_copy(
                    tT_sb[:, j // GR, :, j % GR * P:(j % GR + 1) * P],
                    ps_tT[j % XR][:, :].rearrange("p (k c) -> p k c", k=KH)).then_inc(tT_odd_ok, 1)

            for j in range(1, GR, 2):
                tT_copy(j)
            for g in range(NG):
                if g < NG - 1:
                    tT_copy((g + 1) * GR + 1)
                xrT_copy(g)
                if g < NG - 1:
                    tT_copy((g + 1) * GR + 3)
                xr_sum(g)
                if g < NG - 1:
                    diagonal(g)
            for h in range(2):
                gates(h)
            dve.wait_ge(consts, CONSTS)
            link(nc.vector.tensor_copy(choice[:, :, :],
                                       i8[:, :, 0:TOP].rearrange("p j c -> p c j")))
            ch = choice[:, :, :].rearrange("p c j -> p (c j)")
            nc.vector.tensor_tensor(oh[:, :, :], iota_e[:, :].unsqueeze(2).broadcast_to([P, E, A]),
                                    ch.unsqueeze(1).broadcast_to([P, E, A]),
                                    ALU.is_equal).then_inc(oh_ok, 1)
            nc.vector.tensor_copy(xf_sb[:, :, H:HG], gate[:, :, :]).then_inc(gate_cols_ok, 1)
            dve.wait_ge(rank_ps, 1)
            EA = E * A
            within, total = ps_rank[:, 0:EA], ps_rank[:, EA:2 * EA]

            def flat(t):
                return t[:, :, :].rearrange("p e a -> p (e a)")

            link(nc.vector.tensor_tensor_scan(flat(run), flat(carry), total, 0.0,
                                              ALU.mult, ALU.add))
            nc.vector.tensor_scalar(more[:, :].unsqueeze(2), run[0:1, :, A - 1:A],
                                    -float((TPE - 1) * P), 0.0,
                                    ALU.add, ALU.max).then_inc(more_ok, 1)
            dve.wait_ge(more_ok, 1)
            link(nc.vector.tensor_tensor(flat(run), flat(run), total, ALU.subtract))
            link(nc.vector.tensor_tensor(flat(rk), flat(run), within, ALU.add))
            link(nc.vector.tensor_tensor(flat(rk), flat(rk), flat(oh), ALU.mult))
            link(nc.vector.reduce_sum(r1[:, :], rk[:, :, :].rearrange("p e a -> p a e"), AX))
            nc.vector.tensor_scalar(over[:, :], r1[:, :], float(CAP), float(FAR),
                                    ALU.is_gt, ALU.mult)
            link(nc.vector.scalar_tensor_tensor(slot_f[:, :], ch, float(CAP), r1[:, :],
                                                ALU.mult, ALU.add))
            link(nc.vector.scalar_tensor_tensor(slot[:, :], over[:, :], -1.0, slot_f[:, :],
                                                ALU.add, ALU.add))
            nc.vector.tensor_scalar(slot_i[:, 0, :], slot[:, :], P.bit_length() - 1, None,
                                    ALU.arith_shift_right)
            link(nc.vector.tensor_scalar(slot_i[:, 1, :], slot[:, :], P - 1, None, ALU.bitwise_and))
            nc.vector.tensor_copy(slot_tp[:, :, :], slot_i[:, :, :]).then_inc(slot_ok, 1)
            dve.wait_ge(slot_ok, 1)
            toks = token1[:, :, :].rearrange("p c j -> p (c j)")
            AQ = A // 4
            for q in range(4):
                a = slice(q * AQ, (q + 1) * AQ)
                wide = [P, AQ, NT]
                link(nc.vector.tensor_tensor(
                    pick_t[:, a, :], iota_t[:, :].unsqueeze(1).broadcast_to(wide),
                    slot_tp[:, 0, a].unsqueeze(2).broadcast_to(wide), ALU.is_equal))
                last = nc.vector.tensor_tensor(what[:, a, :], pick_t[:, a, :],
                                               toks[:, a].unsqueeze(2).broadcast_to(wide), ALU.mult)
                b = slice(q * AQ, min((q + 1) * AQ, A - POOL_PICKS))
                if b.start < b.stop:
                    wide = [P, b.stop - b.start, P]
                    last = nc.vector.tensor_tensor(
                        pick_p[:, b, :], iota_p[:, :].unsqueeze(1).broadcast_to(wide),
                        slot_tp[:, 1, b].unsqueeze(2).broadcast_to(wide), ALU.is_equal)
                last.then_inc(pick_ok, 1)
            dve.wait_ge(slot_ps, 1)
            link(nc.vector.tensor_copy(got[:, :], ps_slot[:, 0:NT]))
            nc.vector.tensor_scalar(src_row[:, :], got[:, :], -1.0, 0.0, ALU.add,
                                    ALU.max).then_inc(lists_ok, 1)
            link(nc.vector.scalar_tensor_tensor(empty[:, :], got[:, :], 0.0, spare[:, :],
                                                ALU.is_equal, ALU.mult))
            nc.vector.scalar_tensor_tensor(dst_row[:, :], got[:, :], -1.0, empty[:, :], ALU.add,
                                           ALU.add).then_inc(lists_ok, 1)

            def w0_low(u):
                a, b = UNIT[u]
                dve.wait_ge(whi_ok, u + 1)
                nc.vector.tensor_tensor(wlo[:, 0, a:b], raw[:, a:b], whi[:, 0, a:b].bitcast(F32),
                                        ALU.subtract).then_inc(wlo0_ok, 1)

            for u in range(KH):
                w0_low(u)

            def x_low(i, s, n):
                b = x_buffer(s)
                dve.wait_ge(xhi_ok, tile(i, s) + 1)
                nc.vector.tensor_tensor(xlo[:, b, :], ps_xT[:, :], xhi[:, b, :].bitcast(F32),
                                        ALU.subtract).then_inc(xlo_ok, n)

            def next_w_low(i, s):
                if 1 <= known(i, s) <= NT - TPE:
                    a, b = UNIT[(s - 1) % NU]
                    half = ((s - 1) // NU + 1) % 2
                    dve.wait_ge(whi_ok, tile(i, s) + NU)
                    nc.vector.tensor_tensor(wlo[:, half, a:b], raw[:, a:b],
                                            whi[:, half, a:b].bitcast(F32),
                                            ALU.subtract).then_inc(wlo_ok, 1)

            def step(i, s, n):
                if known(i, s) + n < NT:
                    x_low(i, s + n, n)
                dve.wait_ge(silu_ok, tile(i, s) + 1)
                nc.vector.tensor_tensor(h_sb[:, 0:I], g_sb[:, :], ps_up[:, 0:I],
                                        ALU.mult).then_inc(h_ok, n)
                for t in range(s, s + n):
                    next_w_low(i, t)
                dve.wait_ge(hhi_ok, tile(i, s) + 1)
                nc.vector.tensor_tensor(hlo[:, :], ps_hT[:, 0:IP], hhi[:, :].bitcast(F32),
                                        ALU.subtract).then_inc(hlo_ok, n)

            x_low(0, 0, 1)
            w0_low(KH)
            over_slots(dve, step)

        @block.tensor
        def _(pe):
            def x_tile_turn(j):
                pe.wait_ge(x_in[j // 2], 16)
                if j >= XR:
                    pe.wait_ge((tT_even_ok, tT_odd_ok)[j % 2], (j - XR) // 2 + 1)
                for k in range(KH):
                    last = nc.tensor.transpose(ps_tT[j % XR][:, k * P:(k + 1) * P],
                                               x_sb[:, j, k * P:(k + 1) * P], ident[:, :])
                last.then_inc(tT_ps, 1)

            def router(g):
                pe.wait_ge(tT_even_ok, (g + 1) * (GR // 2))
                pe.wait_ge(tT_odd_ok, (g + 1) * (GR // 2))
                if g >= 1:
                    pe.wait_ge(xrT_ok, g)
                for k in range(KH):
                    last = nc.tensor.matmul(ps_xrT[k * Q:(k + 1) * Q, :], wr_sb[:, k, :],
                                            tT_sb[:, g, k, :], start=True, stop=True)
                last.then_inc(xrT_ps, 1)

            def turn(g):
                pe.wait_ge(xrT_ok, g + 1)
                if g >= 1:
                    pe.wait_ge(xr_ok, g)
                for j in range(GR):
                    last = nc.tensor.transpose(ps_xr[:, j * P:(j + 1) * P],
                                               xrT[:, g, j * P:(j + 1) * P], ident[:, :])
                last.then_inc(xr_ps, 1)

            def logits(g):
                pe.wait_ge(xr_ok, g + 1)
                if g < NG - 1:
                    pe.wait_ge(wbd_ok, 2 * (g + 1))
                else:
                    pe.wait_ge(wbd_last_ok, 2)
                for j in range(g * GR, (g + 1) * GR):
                    c = j % HALF * E
                    last = nc.tensor.matmul(ps_lg[j // HALF][:, c:c + E], wbd[:, j, :], xr[:, j, :],
                                            start=True, stop=True)
                last.then_inc(lg_ps, 1)

            def condition(j):
                pe.wait_ge(x_in[j // 2], 16)
                if j >= XR:
                    pe.wait_ge(xf_ok, j - XR + 1)
                nc.tensor.matmul(ps_xf[j % XR][:, :], wbd[:, j, :], x_sb[:, j, :],
                                 start=True, stop=True).then_inc(xf_ps, 1)

            pe.wait_ge(consts, 4)
            for j in range(GR):
                x_tile_turn(j)
            pe.wait_ge(wr_in, 16)
            for g in range(NG):
                if g < NG - 1:
                    x_tile_turn((g + 1) * GR)
                    x_tile_turn((g + 1) * GR + 1)
                router(g)
                if g < NG - 1:
                    x_tile_turn((g + 1) * GR + 2)
                    x_tile_turn((g + 1) * GR + 3)
                if g == NG - 1:
                    logits(0)
                turn(g)
            for g in range(1, NG):
                logits(g)
                condition(g - 1)
            for j in range(NG - 1, BEFORE_RANKS):
                condition(j)
            pe.wait_ge(consts, CONSTS)
            pe.wait_ge(oh_ok, 1)
            o = oh[:, :, :].rearrange("p e a -> p (e a)")
            nc.tensor.matmul(ps_rank[:, 0:E * A], upper[:, :], o, start=True, stop=True)
            nc.tensor.matmul(ps_rank[:, E * A:2 * E * A], ones[:, :], o,
                             start=True, stop=True).then_inc(rank_ps, 1)
            for j in range(BEFORE_RANKS, TT):
                condition(j)
            for a in range(A):
                if a % (A // 4) == 0:
                    pe.wait_ge(pick_ok, a // (A // 4) + 1)
                if a >= A - POOL_PICKS:
                    pe.wait_ge(pool_pick_ok, a - (A - POOL_PICKS) + 1)
                last = nc.tensor.matmul(ps_slot[:, 0:NT], pick_p[:, a, :], what[:, a, :],
                                        start=(a == 0), stop=(a == A - 1))
            last.then_inc(slot_ps, 1)
            for _ in range(KEEP_WARM):
                nc.tensor.matmul(ps_hT[:, :], ident[:, :], x_sb[:, 0, :], start=True, stop=True)

            pe.wait_ge(xf_ok, TT)

            def x_turn(i, s, n):
                pe.wait_ge(xg_in[s % TPE], (expert(i, s) + 1) * 16)
                if known(i, s) > 0:
                    pe.wait_ge(xlo_ok, tile(i, s) - n + 1)
                for k in range(KH):
                    last = nc.tensor.transpose(ps_xT[:, k * P:(k + 1) * P],
                                               xg[:, s % TPE, k * P:(k + 1) * P], ident[:, :])
                last.then_inc(xT_ps, n)

            def gate_up(i, s, n, ks):
                half, b = half_of(s), x_buffer(s)
                for left, rights in ((xhi, (whi, wlo)), (xlo, (whi,))):
                    if 0 in ks:
                        pe.wait_ge(xhi_ok if left is xhi else xlo_ok, tile(i, s) + 1)
                    for k in ks:
                        g, u = UNIT[k][0], UNIT[k][0] + I
                        c = slice(k * P, (k + 1) * P)
                        for right in rights:
                            for ps, o in ((ps_gate, g), (ps_up, u)):
                                last = nc.tensor.matmul(
                                    ps[:, 0:I], left[:, b, c], right[:, half, o:o + I],
                                    start=(k == 0 and left is xhi and right is whi),
                                    stop=(k == KH - 1 and left is xlo))
                if KH - 1 in ks:
                    last.then_inc(gu_ps, n)

            def down(i, s, n):
                half = half_of(s)
                pe.wait_ge(hlo_ok, tile(i, s) + 1)
                if known(i, s) == 0:
                    pe.wait_ge(wlo0_ok, NU)
                elif s % TPE == 0:
                    pe.wait_ge(wlo_ok, tile(i, s))
                if known(i, s) > 0:
                    pe.wait_ge(y_ok, tile(i, s))
                for c in range(KI):
                    o = DOWN + c * H
                    for q, (left, right) in enumerate(((hhi, whi), (hhi, wlo), (hlo, whi))):
                        last = nc.tensor.matmul(ps_y[:, :], left[:, c * P:(c + 1) * P],
                                                right[:, half, o:o + H],
                                                start=(c == 0 and q == 0),
                                                stop=(c == KI - 1 and q == 2))
                last.then_inc(y_ps, n)

            def step(i, s, n):
                if known(i, s) == 0:
                    pe.wait_ge(wlo0_ok, KH)
                elif s % TPE == 0:
                    pe.wait_ge(wlo_ok, tile(i, s) - NU + 2)
                gate_up(i, s, n, (0, 1))
                if known(i, s) + n < NT:
                    x_turn(i, s + n, n)
                if s % TPE == 0 and known(i, s) > 0:
                    pe.wait_ge(wlo_ok, tile(i, s) - 1)
                gate_up(i, s, n, (2, 3))
                if known(i, s) > 0:
                    tile_before(pe, i, s, down)
                pe.wait_ge(h_ok, tile(i, s) + 1)
                for c in range(KI):
                    last = nc.tensor.transpose(ps_hT[:, c * P:(c + 1) * P],
                                               h_sb[:, c * P:(c + 1) * P], ident[:, :])
                last.then_inc(hT_ps, n)

            pe.wait_ge(more_ok, 1)
            x_turn(0, 0, 1)
            over_slots(pe, step)
            tile_before(pe, PASSES, NT - PASS * PASSES, down)


def kernel(x, itok_B_1_198, L0_cond_weights, L0_ffn_Wr, L0_ffn_Wg, L0_ffn_Wu, L0_ffn_Wd):
    import numpy as np
    import concourse.bacc as bacc
    from concourse.bass_utils import run_bass_kernel_spmd

    arrays = {
        "x": np.asarray(x).reshape(B * C, H),
        "cond": np.asarray(itok_B_1_198).reshape(TT, 2).T,
        "wcond": np.asarray(L0_cond_weights).reshape(S * C, D),
        "wr": np.asarray(L0_ffn_Wr).T,
        "wgu": np.concatenate([np.asarray(w).transpose(0, 2, 1) for w in (L0_ffn_Wg, L0_ffn_Wu)],
                              axis=2),
        "wd": np.asarray(L0_ffn_Wd).transpose(0, 2, 1),
    }
    arrays = {name: np.ascontiguousarray(a) for name, a in arrays.items()}
    nc = bacc.Bacc("TRN2", target_bir_lowering=False, num_devices=1)
    ins = [nc.dram_tensor(name, a.shape, mybir.dt.from_np(a.dtype), kind="ExternalInput").ap()
           for name, a in arrays.items()]
    out = nc.dram_tensor("out", (N + CAP, H), F32, kind="ExternalOutput").ap()
    build(nc, *ins, out)
    r = run_bass_kernel_spmd(nc, [arrays], core_ids=[0])
    return r.results[0]["out"][0:N].reshape(B, C, H)
```
